# Optimizing a Trainium2 kernel written in Bass

```python
import numpy as np
import jax
import jax.numpy as jnp

def _softmax(x, axis=-1):
    return jax.nn.softmax(x, axis=axis)

def _gelu(x):
    return jax.nn.gelu(x, approximate=True)

def _silu(x):
    return jax.nn.silu(x)

def _sigmoid(x):
    return jax.nn.sigmoid(x)

def _layernorm(x, axis=-1, eps=1e-05):
    m = jnp.mean(x, axis=axis, keepdims=True)
    v = jnp.var(x, axis=axis, keepdims=True)
    return (x - m) / jnp.sqrt(v + eps)

def _scatter_add(tgt, idx, src, axis=0):
    return tgt.at[idx].add(src)

def _segment_sum(src, seg, n):
    return jax.ops.segment_sum(src, seg, n)
kernel_name = 'mk_seq_postln_d1_jaxref_r8_889007'

def setup_inputs(seed: int=0):
    np.random.seed(seed)
    _w = jnp.asarray

    def _L0_attn_setup():
        import jax, jax.numpy as jnp
        import numpy as np
        D_MODEL = 128
        N_HEADS = 16
        LAMBDA = 0.5
        EPS = 1e-09
        key = jax.random.key(seed)
        ks = jax.random.split(key, 5)
        B, L, D = (2, 256, D_MODEL)
        scale = 1.0 / np.sqrt(D)
        return {'x': jax.random.normal(ks[0], (B, L, D), dtype=jnp.float32), 'Wq': jax.random.normal(ks[1], (D, D), dtype=jnp.float32) * scale, 'bq': jnp.zeros((D,), dtype=jnp.float32), 'Wk': jax.random.normal(ks[2], (D, D), dtype=jnp.float32) * scale, 'bk': jnp.zeros((D,), dtype=jnp.float32), 'Wv': jax.random.normal(ks[3], (D, D), dtype=jnp.float32) * scale, 'bv': jnp.zeros((D,), dtype=jnp.float32), 'Wo': jax.random.normal(ks[4], (D, D), dtype=jnp.float32) * scale, 'bo': jnp.zeros((D,), dtype=jnp.float32)}
    _L0_attn_in = _L0_attn_setup()

    def _L0_ffn_setup():
        import jax, jax.numpy as jnp
        import numpy as np
        JITTER_EPS = 0.01

        def phi_routing(logits, jitter_eps=JITTER_EPS):
            m, sel = jax.lax.top_k(logits, 2)
            T, E = logits.shape
            m1 = m[:, :1]
            factor1 = jnp.maximum(jnp.abs(logits), m1)
            mask1 = (m1 - logits) / factor1 > 2.0 * jitter_eps
            p1 = jax.nn.softmax(jnp.where(mask1, -jnp.inf, logits), axis=-1)
            mult1 = jnp.take_along_axis(p1, sel[:, :1], axis=-1)
            m2 = m[:, 1:2]
            factor2 = jnp.maximum(jnp.abs(logits), m2)
            mask2 = (m2 - logits) / factor2 > 2.0 * jitter_eps
            drop_top1 = jnp.arange(E)[None, :] == sel[:, :1]
            p2 = jax.nn.softmax(jnp.where(mask2 | drop_top1, -jnp.inf, logits), axis=-1)
            mult2 = jnp.take_along_axis(p2, sel[:, 1:2], axis=-1)
            return (jnp.concatenate([mult1, mult2], axis=-1), sel)
        key = jax.random.key(seed)
        k = jax.random.split(key, 5)
        B, S, H, F, E = (1, 64, 128, 512, 8)
        return {'hidden_states': jax.random.normal(k[0], (B, S, H), jnp.float32), 'gate_w': jax.random.normal(k[1], (E, H), jnp.float32) * 0.02, 'w1': jax.random.normal(k[2], (E, F, H), jnp.float32) * 0.02, 'w2': jax.random.normal(k[3], (E, H, F), jnp.float32) * 0.02, 'w3': jax.random.normal(k[4], (E, F, H), jnp.float32) * 0.02}
    _L0_ffn_in = _L0_ffn_setup()
    _d = {'L0_attn_x': _L0_attn_in['x'], 'L0_attn_Wq': _L0_attn_in['Wq'], 'L0_attn_bq': _L0_attn_in['bq'], 'L0_attn_Wk': _L0_attn_in['Wk'], 'L0_attn_bk': _L0_attn_in['bk'], 'L0_attn_Wv': _L0_attn_in['Wv'], 'L0_attn_bv': _L0_attn_in['bv'], 'L0_attn_Wo': _L0_attn_in['Wo'], 'L0_attn_bo': _L0_attn_in['bo'], 'L0_ffn_gate_w': _L0_ffn_in['gate_w'], 'L0_ffn_w1': _L0_ffn_in['w1'], 'L0_ffn_w2': _L0_ffn_in['w2'], 'L0_ffn_w3': _L0_ffn_in['w3']}
    _x0 = _d['L0_attn_x']
    _d['L0_attn_x'] = jax.random.normal(jax.random.fold_in(jax.random.key(seed), 1), (16, 512, 128), dtype=_x0.dtype)
    del _x0
    return _d

def reference(L0_attn_x, L0_attn_Wq, L0_attn_bq, L0_attn_Wk, L0_attn_bk, L0_attn_Wv, L0_attn_bv, L0_attn_Wo, L0_attn_bo, L0_ffn_gate_w, L0_ffn_w1, L0_ffn_w2, L0_ffn_w3):

    def _L0_attn_ref(x, Wq, bq, Wk, bk, Wv, bv, Wo, bo):
        import jax, jax.numpy as jnp
        import numpy as np
        D_MODEL = 128
        N_HEADS = 16
        LAMBDA = 0.5
        EPS = 1e-09
        B, L, D = x.shape
        H = N_HEADS
        dk = D // H

        def heads(y):
            return y.reshape(B, L, H, dk).transpose(0, 2, 1, 3)
        Q = heads(x @ Wq.T + bq)
        K = heads(x @ Wk.T + bk)
        V = heads(x @ Wv.T + bv)
        scores = jnp.einsum('bhqd,bhkd->bhqk', Q, K) / jnp.sqrt(jnp.float32(dk))
        probs = jax.nn.softmax(scores, axis=-1)
        intervened = probs.at[:, :, :, 0].set(0.0)
        denom = jnp.clip(intervened.sum(axis=-1, keepdims=True), 1e-09, None)
        intervened = intervened / denom
        combined = probs + LAMBDA * (intervened - probs)
        attn_out = jnp.einsum('bhqk,bhkd->bhqd', combined, V)
        attn_out = attn_out.transpose(0, 2, 1, 3).reshape(B, L, D)
        return attn_out @ Wo.T + bo

    def _L0_ffn_ref(hidden_states, gate_w, w1, w2, w3):
        import jax, jax.numpy as jnp
        import numpy as np
        JITTER_EPS = 0.01

        def phi_routing(logits, jitter_eps=JITTER_EPS):
            m, sel = jax.lax.top_k(logits, 2)
            T, E = logits.shape
            m1 = m[:, :1]
            factor1 = jnp.maximum(jnp.abs(logits), m1)
            mask1 = (m1 - logits) / factor1 > 2.0 * jitter_eps
            p1 = jax.nn.softmax(jnp.where(mask1, -jnp.inf, logits), axis=-1)
            mult1 = jnp.take_along_axis(p1, sel[:, :1], axis=-1)
            m2 = m[:, 1:2]
            factor2 = jnp.maximum(jnp.abs(logits), m2)
            mask2 = (m2 - logits) / factor2 > 2.0 * jitter_eps
            drop_top1 = jnp.arange(E)[None, :] == sel[:, :1]
            p2 = jax.nn.softmax(jnp.where(mask2 | drop_top1, -jnp.inf, logits), axis=-1)
            mult2 = jnp.take_along_axis(p2, sel[:, 1:2], axis=-1)
            return (jnp.concatenate([mult1, mult2], axis=-1), sel)
        B, S, H = hidden_states.shape
        E = w1.shape[0]
        x = hidden_states.reshape(-1, H)
        logits = x @ gate_w.T
        routing_weights, selected = phi_routing(logits)
        T = x.shape[0]
        wte = jnp.zeros((T, E), x.dtype).at[jnp.arange(T)[:, None], selected].add(routing_weights)
        out = jnp.zeros_like(x)
        for e in range(E):
            h = jax.nn.silu(x @ w1[e].T) * (x @ w3[e].T)
            out = out + wte[:, e:e + 1] * (h @ w2[e].T)
        return out.reshape(B, S, H)
    x = L0_attn_x
    x = _layernorm(x + _L0_attn_ref(x, L0_attn_Wq, L0_attn_bq, L0_attn_Wk, L0_attn_bk, L0_attn_Wv, L0_attn_bv, L0_attn_Wo, L0_attn_bo), axis=-1)
    x = _layernorm(x + _L0_ffn_ref(x, L0_ffn_gate_w, L0_ffn_w1, L0_ffn_w2, L0_ffn_w3), axis=-1)
    return x

_drawn_inputs = setup_inputs


def setup_inputs(seed=0):
    import zlib

    import numpy as np

    out = dict(_drawn_inputs(seed))
    spreads = {'L0_attn_bq': (0.0, 0.756),
     'L0_attn_bk': (0.0, 0.8),
     'L0_attn_bv': (0.0, 0.1),
     'L0_attn_bo': (0.0, 0.1)}
    factors = {'L0_ffn_gate_w': 3.968, 'L0_ffn_w1': 3.481, 'L0_ffn_w2': 3.463, 'L0_ffn_w3': 3.464}
    for name, (base, spread) in spreads.items():
        noise = np.random.default_rng([zlib.crc32(name.encode()), seed]).standard_normal(out[name].shape)
        drawn = base * np.exp(spread * noise) if base else spread * noise
        out[name] = jnp.asarray(drawn.astype(out[name].dtype))
    for name, factor in factors.items():
        out[name] = (out[name] * factor).astype(out[name].dtype)
    return out
```

```python
from contextlib import ExitStack

import numpy as np

import concourse.bass as bass
from concourse import mybir

P = 128
NB, L, D = 16, 512, 128
NH = 16
DK = D // NH
NT = NB * L
QC = L // P
HG = 4
NG = NH // HG
VW = 32
PARTS = 3
KR = PARTS * PARTS * DK
MR = 2
E, F = 8, 512
FC = F // P
REGION = NT + P
TILES = 2 * NT // P + E
ROW = 132
SKIP = 1 << 20
EPS = 1e-5
JITTER2 = 0.02
SCALE = float(1.0 / np.sqrt(np.float32(DK)))
BIG = 3.0e38


def layer(nc, xT, x, wqT, wkT, wvT, woT, bq, bk, bv, bo, gateT, w1T, w3T, w2T, out):
    f32, bf16, i32 = mybir.dt.float32, mybir.dt.bfloat16, mybir.dt.int32
    ALU, ACT, AXX = mybir.AluOpType, mybir.ActivationFunctionType, mybir.AxisListType.X

    parts_d = nc.dram_tensor("parts_d", [2, 2, PARTS, P, L], bf16).ap()
    negmax_d = nc.dram_tensor("negmax_d", [2, MR, HG * QC, P], bf16).ap()
    x1_d = nc.dram_tensor("x1_d", [NT, D], f32).ap()
    rows_d = nc.dram_tensor("rows_d", [E * REGION + E * P, ROW], f32).ap()
    y_d = nc.dram_tensor("y_d", [2 * NT, D], f32).ap()

    x_b = x.rearrange("(b c p) d -> b p c d", c=QC, p=P)
    x1_b = x1_d.rearrange("(b c p) d -> b p c d", c=QC, p=P)
    out_b = out.rearrange("(b c p) d -> b p c d", c=QC, p=P)
    y_b = y_d.rearrange("(b c p) d -> b p c d", c=QC, p=P)

    ctx = ExitStack()
    with ctx:
        def sb(name, shape, dt=f32):
            return ctx.enter_context(nc.sbuf_tensor(name + "_sb", shape, dt))

        def sem(name):
            return ctx.enter_context(nc.semaphore(name))

        regions = [sb(f"region{n}", [P, E * F]) for n in range(4)]
        QS = [regions[n][:, :].bitcast(bf16).rearrange("p (h q) -> p h q", h=NH) for n in (0, 1)]
        KS = [regions[n][:, :].bitcast(bf16).rearrange("p (h q) -> p h q", h=NH) for n in (2, 3)]
        W1, W3, W2 = regions[0], regions[2], regions[1]
        pt_flat = [sb(f"probs{n}", [P, HG * QC * L]) for n in range(2)]
        PT = [t[:, :].rearrange("p (j c q) -> p j c q", j=HG, c=QC) for t in pt_flat]
        xT_sb = [sb(f"xT{n}", [D, L]) for n in range(2)]
        x_sb = sb("x", [P, QC, D])
        wq_sb, wk_sb, wv_sb, wo_sb = (sb(n, [D, D]) for n in ("wq", "wk", "wv", "wo"))
        woh_sb = sb("wo_half", [D, D])
        bq_sb, bk_sb = sb("bq", [D, 1]), sb("bk", [D, 1])
        bv_sb, bo_sb = sb("bv", [P, D]), sb("bo", [P, D])
        gate_sb = sb("gate", [D, E])
        ident = sb("ident", [P, P])
        upper = sb("upper", [P, P])
        ones = sb("ones", [P, P])
        full = sb("full", [P, L])
        rest = sb("rest", [P, L])
        qk_parts = sb("qk_parts", [P, PARTS, L], bf16)
        VE = [sb(f"values{n}", [P, QC, NH, VW]) for n in range(2)]
        notkey0 = sb("notkey0", [P, 1])
        rowmax = [sb(f"rowmax{n}", [P, HG * QC]) for n in range(2)]
        negmax = sb("negmax", [HG * QC, P])
        negmax_parts = sb("negmax_parts", [HG * QC, MR, P], bf16)
        OT = sb("OT", [P, L])
        TN = sb("TN", [P, NG, QC, HG, VW])
        recips = sb("recips", [P, 2, NG * QC * HG])
        T1, T2 = (sb(n, [P, NG, QC, HG * DK]) for n in ("T1", "T2"))
        attn = sb("attn", [P, QC, D])
        attnT = sb("attnT", [D, QC, P])
        ysum = sb("ysum", [P, QC, D])
        stats = sb("stats", [P, QC, 6])
        meanvar = sb("meanvar", [P, QC, 2])
        vareps, minushalf, rstd = (sb(n, [P, QC]) for n in ("vareps", "minushalf", "rstd"))
        xn = sb("xn", [P, QC, D])
        xnT = sb("xnT", [D, QC, P])
        logits = sb("logits", [P, QC, E])
        rev = sb("rev", [P, QC, E])
        eoff = sb("eoff", [P, E])
        top = [sb(f"top{n}", [P, QC]) for n in range(2)]
        eqm = sb("eqm", [P, QC, E])
        rank = sb("rank", [P, QC])
        H = sb("H", [P, 2, QC, E])
        Hs = sb("Hs", [P, QC, E])
        l2 = sb("l2", [P, QC, E])
        dist = sb("dist", [P, 2, QC, E])
        absl = sb("absl", [P, QC, E])
        factor = sb("factor", [P, 2, QC, E])
        kept = sb("kept", [P, 2, QC, E])
        expd = sb("expd", [P, 2, QC, E])
        wsum = sb("wsum", [P, 2, QC])
        prefix = sb("prefix", [P, 2, QC, E])
        offs = sb("offs", [P, QC + 1, E])
        posf = sb("posf", [P, 2, QC])
        pos = sb("pos", [P, 2, QC], i32)
        dest = sb("dest", [P, 2, QC])
        XE = [sb(f"sent{n}", [P, QC, 2, ROW]) for n in range(2)]
        padrow = sb("padrow", [P, ROW])
        padpos = sb("padpos", [P, E], i32)
        partition = sb("partition", [P, 1])
        tab = sb("tab", [1, 5, TILES])
        tabc = sb("tabc", [1, 4, E])
        tabi = sb("tabi", [1, E], i32)
        row0_i = sb("row0_i", [1, TILES], i32)
        woff_i = sb("woff_i", [1, TILES], i32)

        def psum(name, banks):
            return ctx.enter_context(nc.psum_tensor(name, [P, banks, L], f32))

        st_ps = [psum(f"st_ps{n}", 2) for n in range(2)]
        mx_ps = [psum(f"mx_ps{n}", 1) for n in range(2)]
        acc_ps = psum("acc_ps", 1)
        misc_ps = psum("misc_ps", 1)

        def carve(n, at, words):
            return pt_flat[n][:, at:at + words]

        RING, YRING = 6, 3
        XG = [carve(0, n * ROW, ROW) for n in range(RING)]
        at = RING * ROW
        XGT = [carve(0, at + n * P, P) for n in range(2)]
        at += 2 * P
        SG = [carve(0, at + n * F, F) for n in range(2)]
        at += 2 * F
        HH = [carve(0, at + n * F, F) for n in range(2)]
        at += 2 * F
        HT = [carve(0, at + n * F, F) for n in range(2)]
        at += 2 * F
        YO = [carve(0, at + n * D, D) for n in range(YRING)]
        up_ps = [st_ps[0][:, 0, :], st_ps[0][:, 1, :]]
        lin_ps = [st_ps[1][:, 0, :], st_ps[1][:, 1, :]]
        xgt_ps, ht_ps, y_ps = mx_ps[0][:, 0, :], mx_ps[1][:, 0, :], misc_ps[:, 0, :]
        tabe = pt_flat[1][0:1, 0:2 * TILES * E].rearrange("p (s t e) -> p s t e", s=2, t=TILES)

        def carve3(n, k):
            return carve(1, (n * 4 + k) * L, L).rearrange("p (c d) -> p c d", c=QC)

        Y0, Y1, X1, RES = ([carve3(n, k) for n in range(2)] for k in range(4))

        s_weights, s_weights_last = sem("weights"), 16 * 9
        s_const = sem("constants")
        s_const_dve = sem("constants_dve")
        s_pool_const, s_pad_step = sem("pool_constant"), sem("padding_step")
        s_xT, s_x = sem("xT_loaded"), sem("x_loaded")
        s_qk_ready, s_qk_drained = sem("qk_projected"), sem("qk_drained")
        s_split, s_split_step = sem("qk_split"), sem("qk_split_step")
        s_parts_stored, s_qk_loaded = sem("parts_stored"), sem("qk_loaded")
        s_v_ready, s_v_drained, s_v_step = sem("v_projected"), sem("v_drained"), sem("values_without_key0")
        s_mx_ready, s_mx_done = sem("mx_ready"), sem("mx_done")
        s_mT_ready, s_mT_drained = sem("mT_ready"), sem("mT_drained")
        s_m_split, s_m_split_step = sem("m_split"), sem("m_split_step")
        s_m_stored, s_m_loaded = sem("m_stored"), sem("m_loaded")
        s_st_ready, s_exp_done = sem("st_ready"), sem("exp_done")
        s_pv_ready, s_acc_drained = sem("pv_ready"), sem("acc_drained")
        s_ot_ready, s_ot_drained = sem("ot_ready"), sem("ot_drained")
        s_norm = sem("norm_step")
        s_at_ready, s_at_drained = sem("at_ready"), sem("at_drained")
        s_wo_ready, s_wo_drained = sem("wo_ready"), sem("wo_drained")
        s_xb = sem("x_plus_bo")
        s_ln, s_var, s_rstd = sem("ln_step"), sem("vareps_done"), sem("rstd_done")
        s_xn, s_x1_stored = sem("xn_done"), sem("x1_stored")
        s_xt_ready, s_xt_drained = sem("xt_ready"), sem("xt_drained")
        s_gl_ready, s_gl_drained = sem("gl_ready"), sem("gl_drained")
        s_rt = sem("route_step")
        s_expd = sem("expd_done")
        s_px_ready, s_px_drained = sem("px_ready"), sem("px_drained")
        s_sent_step, s_scattered = sem("sent_x"), sem("scattered")
        s_tab, s_tab_done = sem("table_step"), sem("table_done")
        s_pad = sem("padding_scattered")
        s_w = sem("expert_weights")
        s_xg = [sem(f"xg_loaded{n}") for n in range(RING)]
        s_xgt_ready, s_xgt = sem("xgt_ready"), sem("xgt_drained")
        s_up, s_lin, s_silu, s_h = sem("up_ready"), sem("lin_ready"), sem("silu_done"), sem("h_done")
        s_ht_ready, s_ht = sem("ht_ready"), sem("ht_drained")
        s_y_ready, s_y = sem("y_ready"), sem("y_drained")
        s_y_out = [sem(f"y_scattered{n}") for n in range(YRING)]
        s_f_in = [sem(f"final_loaded{n}") for n in range(2)]
        s_f_sum, s_f_res = sem("final_ysum"), sem("final_res")
        s_f_step, s_f_var, s_f_rstd = sem("final_step"), sem("final_var"), sem("final_rstd")
        s_f_stored = [sem(f"final_stored{n}") for n in range(2)]

        s_lone_sp, s_lone_pool, s_lone_dve = (sem(f"lone_waits_{n}") for n in ("sp", "pool", "dve"))
        s_lone = {}

        def live(b):
            return not isinstance(b, int) or 0 <= b < NB

        def lone_wait(eng, s, n):
            eng.wait_ge(s, n)
            if not isinstance(n, int):
                eng.sem_inc(s_lone[id(eng)], 1)

        def pipeline(eng, iteration):
            for b in range(-2, 2):
                iteration(b, b % 2)
            with eng.Fori(1, NB // 2 - 1) as i:
                iteration(2 * i, 0)
                iteration(2 * i + 1, 1)
            for b in range(NB - 2, NB + 2):
                iteration(b, b % 2)

        def rows_in(n, r):
            return s_xg[n % RING], 16 * (r + n // RING + 1)

        def rows_out(n, r):
            return s_y_out[n % YRING], 16 * (RING // YRING * r + n // YRING + 1)

        def tiles_pipeline(eng, step):
            first = RING
            rounds = (TILES - 1 - first) // RING
            for t in range(-1, first):
                step(t, t % RING, t // RING)
            with eng.Fori(1, 1 + rounds) as i:
                for n in range(RING):
                    step(RING * i + n, n, i)
            for t in range(first + rounds * RING, TILES + 1):
                step(t, t % RING, t // RING)

        SPARE, SENT = 16 * E, 16 * 2 * QC
        NORM, LN, RT = 6, 2 * QC, 33

        block = ctx.enter_context(nc.Block())

        @block.sync
        def _(sp):
            s_lone[id(sp)] = s_lone_sp
            for dst, src in ((wq_sb, wqT), (wk_sb, wkT), (wv_sb, wvT), (wo_sb, woT), (gate_sb, gateT),
                             (bq_sb, bq), (bk_sb, bk)):
                sp.dma_start(dst[:, :], src).then_inc(s_weights, 16)
            sp.dma_start(bv_sb[:, :], bv.to_broadcast([P, D])).then_inc(s_weights, 16)
            sp.dma_start(bo_sb[:, :], bo.to_broadcast([P, D])).then_inc(s_weights, 16)

            def load_xT(b, par):
                if live(b - 2):
                    lone_wait(sp, s_v_ready, b - 1)
                    lone_wait(sp, s_qk_ready, 2 * (b - 1))
                col = b * L
                src = xT[:, col:col + L] if isinstance(b, int) else xT[:, bass.ds(col, L)]
                sp.dma_start(xT_sb[par][:, :], src).then_inc(s_xT, 16)

            def load_x(b):
                if live(b - 1):
                    lone_wait(sp, s_wo_drained, b)
                src = x_b[b] if isinstance(b, int) else x_b[bass.ds(b, 1)].rearrange("o p c d -> (o p) c d")
                sp.dma_start(x_sb[:, :, :], src).then_inc(s_x, 16)

            def store_parts(b, par, which):
                lone_wait(sp, s_split, 2 * b + which + 1)
                if live(b - 2):
                    lone_wait(sp, s_qk_loaded, 16 * 2 * PARTS * PARTS * (b - 1))
                sp.dma_start(parts_d[par, which].rearrange("t p q -> p t q"), qk_parts[:, :, :])\
                  .then_inc(s_parts_stored, 16)

            def load_qk(b, par):
                lone_wait(sp, s_parts_stored, 32 * (b + 1))
                if live(b - 2):
                    lone_wait(sp, s_exp_done, 32 * (b - 1))
                else:
                    sp.wait_ge(s_const, 8)
                for c in range(PARTS * PARTS):
                    for which, dst, part in ((0, QS[par], c // PARTS), (1, KS[par], c % PARTS)):
                        sp.dma_start(dst[DK * c:DK * (c + 1), :, :],
                                     parts_d[par, which, part].rearrange("(h d) q -> d h q", d=DK))\
                          .then_inc(s_qk_loaded, 16)

            def move_negmax(b, bpar, g):
                u = 4 * b + g
                lone_wait(sp, s_m_split, u + 1)
                if not (isinstance(u, int) and u < 2):
                    lone_wait(sp, s_m_loaded, 16 * (u - 1))
                sp.dma_start(negmax_d[g % 2].rearrange("t r q -> r t q"), negmax_parts[:, :, :])\
                  .then_inc(s_m_stored, 16)
                lone_wait(sp, s_m_stored, 16 * (u + 1))
                sp.dma_start(QS[bpar][KR:KR + MR, HG * g:HG * (g + 1), :],
                             negmax_d[g % 2].rearrange("t r q -> t (r q)")
                                            .rearrange("t (h q) -> t h q", h=HG)).then_inc(s_m_loaded, 16)

            def store_x1(b):
                lone_wait(sp, s_xn, b + 1)
                dst = x1_b[b] if isinstance(b, int) else x1_b[bass.ds(b, 1)].rearrange("o p c d -> (o p) c d")
                sp.dma_start(dst, xn[:, :, :]).then_inc(s_x1_stored, 16)

            def iteration(b, par):
                if live(b + 2):
                    load_xT(b + 2, par)
                if live(b - 1):
                    load_x(b - 1)
                if live(b + 1):
                    load_qk(b + 1, 1 - par)
                for g in range(NG):
                    gg, off = (g + 1) % NG, (g + 1) // NG
                    if live(b + off):
                        move_negmax(b + off, (par + off) % 2, gg)
                    if g == 1 and live(b + 2):
                        store_parts(b + 2, par, 0)
                    if g == 3:
                        if live(b + 2):
                            store_parts(b + 2, par, 1)
                        if live(b - 1):
                            store_x1(b - 1)

            pipeline(sp, iteration)

            sp.wait_ge(s_exp_done, 32 * NB)
            for dst, src in ((W1, w1T), (W3, w3T), (W2, w2T)):
                sp.dma_start(dst[:, :], src).then_inc(s_w, 16)
            sp.wait_ge(s_scattered, SPARE + SENT * NB)
            sp.wait_ge(s_pad, 16 * E)
            sp.wait_ge(s_tab_done, 1)
            sp.wait_ge(s_pv_ready, 4 * NB)

            def load_rows(t, n, r):
                if not (isinstance(t, int) and t < RING):
                    lone_wait(sp, *rows_out(n, r - 1))
                at = row0_i[0:1, t:t + 1] if isinstance(t, int) else row0_i[0:1, bass.ds(t, 1)]
                row = sp.value_load(at, min_val=0, max_val=E * REGION + (E - 1) * P)
                sp.dma_start(XG[n], rows_d[bass.ds(row, P), :]).then_inc(s_xg[n], 16)

            for t in range(RING):
                load_rows(t, t, 0)
            with sp.Fori(1, TILES // RING) as i:
                for n in range(RING):
                    load_rows(RING * i + n, n, i)
            for t in range(TILES // RING * RING, TILES):
                load_rows(t, t % RING, t // RING)

            for t in range(TILES - YRING, TILES):
                sp.wait_ge(*rows_out(t % RING, t // RING))
            sp.wait_ge(s_x1_stored, 16 * NB)

            def final_load(b, n):
                if not (isinstance(b, int) and b < 2):
                    lone_wait(sp, s_f_step, 3 * QC * (b - 1))
                for dst, src, k in ((Y0[n], y_b, 0), (Y1[n], y_b, NB), (X1[n], x1_b, 0)):
                    at = src[b + k] if isinstance(b, int) else \
                        src[bass.ds(b + k, 1)].rearrange("o p c d -> (o p) c d")
                    sp.dma_start(dst, at).then_inc(s_f_in[n], 16)

            def final_store(b, n):
                lone_wait(sp, s_f_step, 3 * QC * (b + 1))
                dst = out_b[b] if isinstance(b, int) else out_b[bass.ds(b, 1)].rearrange("o p c d -> (o p) c d")
                sp.dma_start(dst, RES[n]).then_inc(s_f_stored[n], 16)

            final_load(0, 0)
            final_load(1, 1)
            with sp.Fori(0, NB // 2 - 1) as i:
                for n in range(2):
                    final_store(2 * i + n, n)
                    final_load(2 * i + n + 2, n)
            final_store(NB - 2, 0)
            final_store(NB - 1, 1)
            for n in range(2):
                sp.wait_ge(s_f_stored[n], 16 * (NB // 2))

        @block.tensor
        def _(pe):
            pieces = []
            for k in range(16):
                g = k // 4
                if k % 4 == 0:
                    pieces.append((s_mT_drained, (g + 1) // NG, 4, (g + 1) % NG))
                elif k % 4 == 1:
                    pieces.append((s_ot_drained, (g - 2) // NG, 4, (g - 2) % NG))
                else:
                    pieces.append({2: (s_px_drained, -2, 1, 0), 3: (s_qk_drained, 2, 2, 0),
                                   6: (s_v_drained, 1, 1, 0), 7: (s_at_drained, -1, 1, 0),
                                   10: (s_wo_drained, -1, 1, 0), 11: (s_qk_drained, 2, 2, 1),
                                   14: (s_xt_drained, -1, 1, 0), 15: (s_gl_drained, -1, 1, 0)}[k])

            def misc_free(b, k):
                for back in range(1, 32):
                    kk, bb = (k - back) % 16, b + (k - back) // 16
                    s, off, per, n = pieces[kk]
                    if live(bb + off):
                        pe.wait_ge(s, per * (bb + off) + n + 1)
                        return

            def score_half(b, par, g, j, half):
                slot = 16 * b + 4 * g + j
                first = isinstance(b, int) and b == 0 and g == 0 and j == 0
                if not first:
                    pe.wait_ge(s_exp_done, 2 * slot + half - 1)
                h = HG * g + j
                for i in range(2):
                    c = 2 * half + i
                    last = nc.tensor.matmul(st_ps[half][:, i, :], KS[par][0:KR + MR, h, P * c:P * (c + 1)],
                                            QS[par][0:KR + MR, h, :], start=True, stop=True)
                last.then_inc(s_st_ready, 1)

            def max_chunk(b, par, g, j, c):
                n = 64 * b + 16 * g + 4 * j + c
                if not (isinstance(n, int) and n < 2):
                    pe.wait_ge(s_mx_done, n - 1)
                h = HG * g + j
                nc.tensor.matmul(mx_ps[c % 2][:, 0, :], QS[par][0:KR, h, P * c:P * (c + 1)],
                                 KS[par][0:KR, h, :], start=True, stop=True).then_inc(s_mx_ready, 1)

            def values(b, par, g, j):
                u = 4 * b + g
                if j == 0:
                    if not (isinstance(u, int) and u == 0):
                        pe.wait_ge(s_acc_drained, u)
                    pe.wait_ge(s_exp_done, 8 * (u + 1))
                    pe.wait_ge(s_v_step, 2 * (b + 1))
                for hj in range(HG):
                    last = nc.tensor.matmul(acc_ps[32 * hj:32 * hj + VW, 0, :],
                                            VE[par][:, j, HG * g + hj, :], PT[g % 2][:, hj, j, :],
                                            start=(j == 0), stop=(j == QC - 1))
                if j == QC - 1:
                    last.then_inc(s_pv_ready, 1)

            def project_qk(b, par, which):
                pe.wait_ge(s_xT, 16 * (b + 1))
                nc.tensor.matmul(misc_ps[:, 0, :], (wq_sb, wk_sb)[which][:, :], xT_sb[par][:, :],
                                 start=True, stop=True).then_inc(s_qk_ready, 1)

            def project_v(par):
                for c in range(QC):
                    last = nc.tensor.matmul(misc_ps[:, 0, P * c:P * (c + 1)], xT_sb[par][:, P * c:P * (c + 1)],
                                            wv_sb[:, :], start=True, stop=True)
                last.then_inc(s_v_ready, 1)

            def max_to_rows(b, g):
                pe.wait_ge(s_mx_done, 16 * (4 * b + g + 1))
                nc.tensor.transpose(misc_ps[0:HG * QC, 0, 0:P], rowmax[g % 2][:, :], ident[:, :])\
                  .then_inc(s_mT_ready, 1)

            def sums_by_query(b, g):
                pe.wait_ge(s_acc_drained, 4 * b + g + 1)
                for c in range(QC):
                    last = nc.tensor.transpose(misc_ps[:, 0, P * c:P * (c + 1)], OT[:, P * c:P * (c + 1)],
                                               ident[:, :])
                last.then_inc(s_ot_ready, 1)

            def chunks_transposed(src, ready):
                for c in range(QC):
                    last = nc.tensor.transpose(misc_ps[:, 0, P * c:P * (c + 1)], src[:, c, :], ident[:, :])
                last.then_inc(ready, 1)

            def misc(b, par, k):
                s, off, per, n = pieces[k]
                bb = b + off
                if not live(bb):
                    return
                misc_free(b, k)
                g = k // 4
                if k % 4 == 0:
                    max_to_rows(bb, (g + 1) % NG)
                elif k % 4 == 1:
                    sums_by_query(bb, (g - 2) % NG)
                elif k == 2:
                    pe.wait_ge(s_rt, RT * bb + 12)
                    nc.tensor.matmul(misc_ps[:, 0, 0:QC * E], upper[:, :], Hs[:, :, :], start=True, stop=True)
                    nc.tensor.matmul(misc_ps[:, 0, QC * E:2 * QC * E], ones[:, :], Hs[:, :, :],
                                     start=True, stop=True).then_inc(s_px_ready, 1)
                elif k in (3, 11):
                    project_qk(bb, par, k == 11)
                elif k == 6:
                    project_v(1 - par)
                elif k == 7:
                    pe.wait_ge(s_norm, NORM * (bb + 1))
                    chunks_transposed(attn, s_at_ready)
                elif k == 10:
                    pe.wait_ge(s_at_drained, bb + 1)
                    for c in range(QC):
                        last = nc.tensor.matmul(misc_ps[:, 0, P * c:P * (c + 1)], attnT[:, c, :],
                                                woh_sb[:, :], start=True, stop=True)
                    last.then_inc(s_wo_ready, 1)
                elif k == 14:
                    pe.wait_ge(s_xn, bb + 1)
                    chunks_transposed(xn, s_xt_ready)
                elif k == 15:
                    pe.wait_ge(s_xt_drained, bb + 1)
                    for c in range(QC):
                        last = nc.tensor.matmul(misc_ps[:, 0, E * c:E * (c + 1)], xnT[:, c, :],
                                                gate_sb[:, :], start=True, stop=True)
                    last.then_inc(s_gl_ready, 1)

            def iteration(b, par):
                for k in range(16):
                    g, j = k // 4, k % 4
                    ahead, ga = (g + 2) // NG, (g + 2) % NG
                    behind, gb = (g - 1) // NG, (g - 1) % NG
                    if j == 0 and live(b):
                        pe.wait_ge(s_m_loaded, 16 * (4 * b + g + 1))
                    if live(b + ahead) and ga == 0 and j == 0:
                        pe.wait_ge(s_qk_loaded, 16 * 2 * PARTS * PARTS * (b + ahead + 1))

                    def chunk(c):
                        if live(b + ahead):
                            max_chunk(b + ahead, (par + ahead) % 2, ga, j, c)

                    chunk(0)
                    if live(b):
                        score_half(b, par, g, j, 0)
                    chunk(1)
                    if live(b + behind):
                        values(b + behind, (par + behind) % 2, gb, j)
                    chunk(2)
                    if live(b):
                        score_half(b, par, g, j, 1)
                    chunk(3)
                    misc(b, par, k)

            pe.wait_ge(s_weights, s_weights_last)
            pe.wait_ge(s_const, 8)
            pe.wait_ge(s_const_dve, 2)
            pipeline(pe, iteration)

            pe.wait_ge(s_tab_done, 1)
            pe.wait_ge(s_w, 16 * 3)
            pe.wait_ge(s_exp_done, 32 * NB)

            carried = [pe.alloc_register(f"expert_offset{n}") for n in range(2)]
            limits = dict(min_val=0, max_val=(E - 1) * F)
            offsets = {}

            def load_offset(t, n):
                at = woff_i[0:1, t:t + 1] if isinstance(t, int) else woff_i[0:1, bass.ds(t, 1)]
                if n % RING == 0:
                    pe.reg_load(carried[0], at)
                else:
                    offsets[n] = pe.value_load(at, **limits)

            def weights(w, n, at, width):
                return w[:, bass.ds(offsets[n % RING] + at, width)]

            def inside(t):
                return not isinstance(t, int) or 0 <= t < TILES

            def step(t, n, r):
                if n == 0:
                    offsets[0] = pe.snap(carried[0], **limits)
                    if not (isinstance(t, int) and t == 0):
                        offsets[RING - 1] = pe.snap(carried[1], **limits)
                if inside(t):
                    pe.wait_ge(s_xgt, t + 1)
                    nc.tensor.matmul(up_ps[n % 2], XGT[n % 2], weights(W1, n, 0, F), start=True, stop=True)\
                      .then_inc(s_up, 1)
                if inside(t - 1):
                    pe.wait_ge(s_h, t)
                    for c in range(FC):
                        last = nc.tensor.transpose(ht_ps[:, P * c:P * (c + 1)],
                                                   HH[(n - 1) % 2][:, P * c:P * (c + 1)], ident[:, :])
                    last.then_inc(s_ht_ready, 1)
                if inside(t + 1):
                    pe.wait_ge(*rows_in(n + 1, r))
                    nc.tensor.transpose(xgt_ps[:, 0:P], XG[(n + 1) % RING][:, 0:P], ident[:, :])\
                      .then_inc(s_xgt_ready, 1)
                if inside(t):
                    nc.tensor.matmul(lin_ps[n % 2], XGT[n % 2], weights(W3, n, 0, F), start=True, stop=True)\
                      .then_inc(s_lin, 1)
                if inside(t + 1):
                    load_offset(t + 1, n + 1)
                if inside(t - 1):
                    pe.wait_ge(s_ht, t)
                    if not (isinstance(t, int) and t < 2):
                        pe.wait_ge(s_y, t - 1)
                    for c in range(FC):
                        last = nc.tensor.matmul(y_ps[:, 0:D], HT[(n - 1) % 2][:, P * c:P * (c + 1)],
                                                weights(W2, n - 1, c * D, D), start=(c == 0), stop=(c == FC - 1))
                    last.then_inc(s_y_ready, 1)
                if n == RING - 1 and not (isinstance(t, int) and t < 0):
                    pe.reg_mov(carried[1], offsets[n])

            tiles_pipeline(pe, step)

        @block.scalar
        def _(act):
            act.wait_ge(s_weights, s_weights_last)
            nc.scalar.activation(woh_sb[:, :], wo_sb[:, :], ACT.Copy, scale=0.5).then_inc(s_const, 1)

            def exp_half(b, g, j, half):
                u = 4 * b + g
                if j == 0 and half == 0 and not (isinstance(u, int) and u < 2):
                    act.wait_ge(s_pv_ready, u - 1)
                act.wait_ge(s_st_ready, 2 * (16 * b + 4 * g + j) + half + 1)
                nc.scalar.activation(PT[g % 2][:, j, 2 * half:2 * half + 2, :], st_ps[half][:, :, :],
                                     ACT.Exp, scale=SCALE).then_inc(s_exp_done, 1)

            def drain_sums(b, g):
                u = 4 * b + g
                act.wait_ge(s_pv_ready, u + 1)
                if not (isinstance(u, int) and u == 0):
                    act.wait_ge(s_ot_ready, u)
                nc.scalar.activation(OT[:, :], acc_ps[:, 0, :], ACT.Copy).then_inc(s_acc_drained, 1)

            def drain(b, k):
                g = k // 4
                if k % 4 == 0:
                    bb, gg = b + (g + 1) // NG, (g + 1) % NG
                    if live(bb):
                        u = 4 * bb + gg
                        act.wait_ge(s_mT_ready, u + 1)
                        if not (isinstance(u, int) and u == 0):
                            act.wait_ge(s_m_split, u)
                        nc.scalar.activation(negmax[:, :], misc_ps[0:HG * QC, 0, 0:P], ACT.Copy, scale=-1.0)\
                          .then_inc(s_mT_drained, 1)
                elif k % 4 == 1:
                    bb, gg = b + (g - 2) // NG, (g - 2) % NG
                    if live(bb):
                        act.wait_ge(s_ot_ready, 4 * bb + gg + 1)
                        if gg == 0 and live(bb - 1):
                            act.wait_ge(s_norm, NORM * bb)
                        nc.scalar.activation(TN[:, gg, :, :, :], misc_ps[:, 0, :]
                                             .rearrange("p (c j v) -> p c j v", c=QC, j=HG), ACT.Copy)\
                          .then_inc(s_ot_drained, 1)
                elif k == 2 and live(b - 2):
                    act.wait_ge(s_px_ready, b - 1)
                    nc.scalar.activation(prefix[:, :, :, :], misc_ps[:, 0, 0:2 * QC * E]
                                         .rearrange("p (s c e) -> p s c e", s=2, c=QC), ACT.Copy)\
                      .then_inc(s_px_drained, 1)
                elif k in (3, 11) and live(b + 2):
                    which = int(k == 11)
                    n = 2 * (b + 2) + which
                    act.wait_ge(s_qk_ready, n + 1)
                    if not (isinstance(n, int) and n == 0):
                        act.wait_ge(s_split, n)
                    nc.scalar.activation(full[:, :], misc_ps[:, 0, :], ACT.Identity,
                                         bias=(bq_sb, bk_sb)[which][:, 0:1]).then_inc(s_qk_drained, 1)
                elif k == 7 and live(b - 1):
                    act.wait_ge(s_at_ready, b)
                    nc.scalar.activation(attnT[:, :, :], misc_ps[:, 0, :].rearrange("p (c q) -> p c q", c=QC),
                                         ACT.Copy).then_inc(s_at_drained, 1)
                elif k == 14 and live(b - 1):
                    act.wait_ge(s_xt_ready, b)
                    nc.scalar.activation(xnT[:, :, :], misc_ps[:, 0, :].rearrange("p (c q) -> p c q", c=QC),
                                         ACT.Copy).then_inc(s_xt_drained, 1)
                elif k == 15 and live(b - 1):
                    act.wait_ge(s_gl_ready, b)
                    if live(b - 2):
                        act.wait_ge(s_rt, RT * (b - 1))
                    nc.scalar.activation(logits[:, :, :], misc_ps[:, 0, 0:QC * E]
                                         .rearrange("p (c e) -> p c e", c=QC), ACT.Copy).then_inc(s_gl_drained, 1)

            def iteration(b, par):
                for k in range(16):
                    g, j = k // 4, k % 4
                    if j == 0 and live(b + (g - 2) // NG):
                        drain_sums(b + (g - 2) // NG, (g - 2) % NG)
                    if live(b):
                        exp_half(b, g, j, 0)
                        exp_half(b, g, j, 1)
                    drain(b, k)
                    if k == 2 and live(b - 2):
                        act.wait_ge(s_rt, RT * (b - 2) + 14)
                        nc.scalar.activation(expd[:, :, :, :], dist[:, :, :, :], ACT.Exp, scale=-1.0)\
                          .then_inc(s_expd, 1)

            pipeline(act, iteration)

            def step(t, n, r):
                def inside(t):
                    return not isinstance(t, int) or 0 <= t < TILES

                if inside(t):
                    act.wait_ge(s_up, t + 1)
                    nc.scalar.activation(SG[n % 2], up_ps[n % 2], ACT.Silu).then_inc(s_silu, 1)
                if inside(t - 1):
                    act.wait_ge(s_ht_ready, t)
                    nc.scalar.activation(HT[(n - 1) % 2], ht_ps[:, :], ACT.Copy).then_inc(s_ht, 1)
                if inside(t + 1):
                    act.wait_ge(s_xgt_ready, t + 2)
                    nc.scalar.activation(XGT[(n + 1) % 2], xgt_ps[:, 0:P], ACT.Copy).then_inc(s_xgt, 1)

            tiles_pipeline(act, step)

        @block.vector
        def _(dve):
            s_lone[id(dve)] = s_lone_dve
            V = nc.vector
            for n in range(2):
                V.memset(KS[n][64:P, :, :], 1.0).then_inc(s_const, 1)
            dve.wait_ge(s_const, 8)
            V.tensor_copy(offs[:, 0, :], eoff[:, :]).then_inc(s_const_dve, 1)
            V.memset(padrow[:, D:D + 1].bitcast(i32), SKIP).then_inc(s_const_dve, 1)

            def after_step(s, n):
                dve.wait_ge(s, n)

            def iteration(b, par):
                count = [0]

                def next_max():
                    k, c = divmod(count[0], QC)
                    count[0] += 1
                    g, j = k // 4, k % 4
                    bb, ga = b + (g + 2) // NG, (g + 2) % NG
                    if not live(bb):
                        return
                    u = 4 * bb + ga
                    if j == 0 and c == 0 and not (isinstance(u, int) and u < 2):
                        dve.wait_ge(s_mT_ready, u - 1)
                    n = 16 * u + 4 * j + c
                    dve.wait_ge(s_mx_ready, n + 1)
                    V.tensor_reduce(rowmax[ga % 2][:, 4 * j + c:4 * j + c + 1], mx_ps[c % 2][:, 0, :],
                                    axis=AXX, op=ALU.max).then_inc(s_mx_done, 1)

                rb = b - 2
                route = live(rb)
                H1, H2 = H[:, 0, :, :], H[:, 1, :, :]

                def rt(n):
                    dve.wait_ge(s_rt, RT * rb + n)

                def per_chunk(x):
                    return x[:, :].unsqueeze(2).to_broadcast([P, QC, E])

                next_max()
                if route:
                    dve.wait_ge(s_gl_drained, rb + 1)
                    V.tensor_reduce(top[0][:, :], logits[:, :, :], axis=AXX, op=ALU.max).then_inc(s_rt, 1)
                next_max()
                if route:
                    rt(1)
                    V.tensor_tensor(eqm[:, :, :], logits[:, :, :], per_chunk(top[0]), ALU.is_equal).then_inc(s_rt, 1)
                    rt(2)
                    V.tensor_tensor(absl[:, :, :], eqm[:, :, :], rev[:, :, :], ALU.mult).then_inc(s_rt, 1)
                next_max()
                if route:
                    rt(3)
                    V.tensor_reduce(rank[:, :], absl[:, :, :], axis=AXX, op=ALU.max).then_inc(s_rt, 1)
                    rt(4)
                    V.tensor_tensor(H1, absl[:, :, :], per_chunk(rank), ALU.is_equal).then_inc(s_rt, 1)
                next_max()
                if route:
                    rt(5)
                    V.scalar_tensor_tensor(out=l2[:, :, :], in0=H1, scalar=-BIG, in1=logits[:, :, :],
                                           op0=ALU.mult, op1=ALU.add).then_inc(s_rt, 1)
                    rt(6)
                    V.tensor_reduce(top[1][:, :], l2[:, :, :], axis=AXX, op=ALU.max).then_inc(s_rt, 1)
                next_max()
                if route:
                    rt(7)
                    V.tensor_tensor(eqm[:, :, :], l2[:, :, :], per_chunk(top[1]), ALU.is_equal).then_inc(s_rt, 1)
                    rt(8)
                    V.tensor_tensor(absl[:, :, :], eqm[:, :, :], rev[:, :, :], ALU.mult).then_inc(s_rt, 1)
                next_max()
                if route:
                    rt(9)
                    V.tensor_reduce(rank[:, :], absl[:, :, :], axis=AXX, op=ALU.max).then_inc(s_rt, 1)
                    rt(10)
                    V.tensor_tensor(H2, absl[:, :, :], per_chunk(rank), ALU.is_equal).then_inc(s_rt, 1)
                next_max()
                if route:
                    rt(11)
                    V.tensor_tensor(Hs[:, :, :], H1, H2, ALU.add).then_inc(s_rt, 1)
                    V.scalar_tensor_tensor(out=dist[:, 0, :, :], in0=logits[:, :, :], scalar=-1.0,
                                           in1=per_chunk(top[0]), op0=ALU.mult, op1=ALU.add).then_inc(s_rt, 1)
                    V.scalar_tensor_tensor(out=dist[:, 1, :, :], in0=l2[:, :, :], scalar=-1.0,
                                           in1=per_chunk(top[1]), op0=ALU.mult, op1=ALU.add).then_inc(s_rt, 1)
                next_max()
                next_max()
                if route:
                    V.scalar_tensor_tensor(out=absl[:, :, :], in0=logits[:, :, :], scalar=-1.0,
                                           in1=logits[:, :, :], op0=ALU.mult, op1=ALU.max).then_inc(s_rt, 1)
                    rt(15)
                    for s in range(2):
                        V.tensor_tensor(factor[:, s, :, :], absl[:, :, :], per_chunk(top[s]), ALU.max)\
                         .then_inc(s_rt, 1)
                if route:
                    rt(17)
                    V.scalar_tensor_tensor(out=kept[:, :, :, :], in0=factor[:, :, :, :], scalar=JITTER2,
                                           in1=dist[:, :, :, :], op0=ALU.mult, op1=ALU.is_ge).then_inc(s_rt, 1)
                next_max()
                next_max()
                next_max()
                if route:
                    rt(18)
                    dve.wait_ge(s_expd, rb + 1)
                    V.tensor_tensor(factor[:, :, :, :], kept[:, :, :, :], expd[:, :, :, :], ALU.mult)\
                     .then_inc(s_rt, 1)
                next_max()
                if route:
                    rt(19)
                    V.tensor_reduce(wsum[:, :, :], factor[:, :, :, :], axis=AXX, op=ALU.add).then_inc(s_rt, 1)
                    rt(20)
                    if live(rb - 1):
                        dve.wait_ge(s_scattered, SPARE + SENT * rb)
                    V.reciprocal(XE[par][:, :, :, D + 1].rearrange("p c s -> p s c"), wsum[:, :, :])\
                     .then_inc(s_rt, 1)
                    V.tensor_copy(XE[par][:, :, :, D].bitcast(i32).rearrange("p c s -> p s c"), dest[:, :, :])\
                     .then_inc(s_rt, 1)
                next_max()
                if route:
                    rt(22)
                    V.tensor_scalar_add(dest[:, :, :], dest[:, :, :], float(L)).then_inc(s_rt, 1)

                for c in range(QC):
                    next_max()
                    if route:
                        if c == 0:
                            dve.wait_ge(s_px_drained, rb + 1)
                            rt(23)
                        else:
                            rt(23 + c)
                        V.tensor_tensor(offs[:, c + 1, :], offs[:, c, :], prefix[:, 1, c, :], ALU.add)\
                         .then_inc(s_rt, 1)
                next_max()
                if route:
                    rt(27)
                    V.tensor_tensor(l2[:, :, :], prefix[:, 0, :, :], offs[:, 0:QC, :], ALU.add).then_inc(s_rt, 1)
                    rt(28)
                    for s in range(2):
                        V.tensor_tensor(factor[:, s, :, :], H[:, s, :, :], l2[:, :, :], ALU.mult).then_inc(s_rt, 1)
                next_max()
                if route:
                    rt(30)
                    V.tensor_reduce(posf[:, :, :], factor[:, :, :, :], axis=AXX, op=ALU.add).then_inc(s_rt, 1)
                    V.tensor_copy(offs[:, 0, :], offs[:, QC, :]).then_inc(s_rt, 1)
                    rt(32)
                    V.tensor_copy(pos[:, :, :], posf[:, :, :]).then_inc(s_rt, 1)
                nb = b - 1
                norm = live(nb)
                SUMS = TN[:, :, :, :, :].rearrange("p g c j v -> p (g c j) v")
                z, z2 = SUMS[:, :, 2 * DK], SUMS[:, :, 2 * DK + 1]
                r1, r2 = recips[:, 0, :], recips[:, 1, :]

                def by_head(t):
                    return t[:, :, :, :].rearrange("p g c (j d) -> p (g c j) d", d=DK)

                def per_head(r):
                    return r.unsqueeze(2).to_broadcast([P, NG * QC * HG, DK])

                for c in range(QC):
                    next_max()
                next_max()
                if norm:
                    dve.wait_ge(s_ot_drained, 4 * (nb + 1))
                    V.scalar_tensor_tensor(out=r2, in0=z, scalar=1e-9, in1=z2, op0=ALU.mult, op1=ALU.max)\
                     .then_inc(s_norm, 1)
                    V.reciprocal(r1, z).then_inc(s_norm, 1)
                next_max()
                if norm:
                    after_step(s_norm, NORM * nb + 1)
                    V.reciprocal(r2, r2).then_inc(s_norm, 1)
                next_max()
                if norm:
                    after_step(s_norm, NORM * nb + 2)
                    V.tensor_tensor(by_head(T1), SUMS[:, :, 0:DK], per_head(r1), ALU.mult).then_inc(s_norm, 1)
                next_max()
                if norm:
                    after_step(s_norm, NORM * nb + 3)
                    V.tensor_tensor(by_head(T2), SUMS[:, :, DK:2 * DK], per_head(r2), ALU.mult).then_inc(s_norm, 1)
                    after_step(s_norm, NORM * nb + 5)
                    V.tensor_tensor(attn[:, :, :].rearrange("p c (g n) -> p g c n", g=NG), T1[:, :, :, :],
                                    T2[:, :, :, :], ALU.add).then_inc(s_norm, 1)
                vb = b + 1
                next_max()
                if live(vb):
                    dve.wait_ge(s_v_ready, vb + 1)
                    if live(vb - 2):
                        dve.wait_ge(s_pv_ready, 4 * (vb - 1))
                    V.tensor_tensor(VE[1 - par][:, :, :, 0:DK],
                                    misc_ps[:, 0, :].rearrange("p (c h d) -> p c h d", c=QC, h=NH),
                                    bv_sb[:, :].rearrange("p (h d) -> p h d", h=NH).unsqueeze(1)
                                               .to_broadcast([P, QC, NH, DK]), ALU.add).then_inc(s_v_drained, 1)
                for c in range(QC - 1):
                    next_max()
                for c in range(3 * QC):
                    next_max()
                next_max()
                if norm:
                    dve.wait_ge(s_wo_ready, nb + 1)
                    dve.wait_ge(s_xb, nb + 1)
                    V.tensor_tensor(ysum[:, :, :], misc_ps[:, 0, :].rearrange("p (c d) -> p c d", c=QC),
                                    x_sb[:, :, :], ALU.add).then_inc(s_wo_drained, 1)
                for c in range(QC):
                    next_max()
                    if norm:
                        if c == 0:
                            dve.wait_ge(s_wo_drained, nb + 1)
                        V.bn_stats(stats[:, c, :], ysum[:, c, :]).then_inc(s_ln, 1)
                if norm:
                    for c in range(QC):
                        lone_wait(dve, s_ln, LN * nb + c + 1)
                        V.bn_aggr(meanvar[:, c, :], stats[:, c, :]).then_inc(s_ln, 1)
                    dve.wait_ge(s_ln, LN * (nb + 1))
                    V.tensor_scalar_add(vareps[:, :], meanvar[:, :, 1], EPS).then_inc(s_var, 1)
                next_max()
                next_max()
                next_max()
                next_max()
                if norm:
                    dve.wait_ge(s_rstd, nb + 1)
                    if live(nb - 1):
                        dve.wait_ge(s_x1_stored, 16 * nb)
                        dve.wait_ge(s_xt_ready, nb)
                        dve.wait_ge(s_sent_step, 2 * nb)
                    for c in range(QC):
                        last = V.tensor_scalar(xn[:, c, :], ysum[:, c, :], meanvar[:, c, 0:1], rstd[:, c:c + 1],
                                               ALU.subtract, ALU.mult)
                        if c < QC - 1:
                            next_max()
                    last.then_inc(s_xn, 1)
                while count[0] < 64:
                    next_max()

            pipeline(dve, iteration)

            step_of = [0]

            def tb(ins):
                step_of[0] += 1
                ins.then_inc(s_tab, 1)
                dve.wait_ge(s_tab, step_of[0])

            cnt, tiles, cum = tabc[:, 0, :], tabc[:, 1, :], tabc[:, 2, :]
            tile_no, expert, excl, row0, woff = (tab[:, n, :] for n in range(5))
            ge, gn = tabe[:, 0, :, :], tabe[:, 1, :, :]

            def by_tile(x):
                return x.unsqueeze(1).to_broadcast([1, TILES, E])

            dve.wait_ge(s_pv_ready, 4 * NB)
            tb(V.tensor_tensor(cnt, offs[0:1, 0, :], eoff[0:1, :], ALU.subtract))
            tb(V.tensor_scalar_add(cnt, cnt, float(P - 1)))
            tb(V.tensor_copy(tabi[:, :], cnt))
            tb(V.tensor_scalar(tabi[:, :], tabi[:, :], P.bit_length() - 1, None, ALU.logical_shift_right))
            tb(V.tensor_copy(tiles, tabi[:, :]))
            tb(V.tensor_copy(cum[:, 0:1], tiles[:, 0:1]))
            for e in range(1, E):
                tb(V.tensor_tensor(cum[:, e:e + 1], cum[:, e - 1:e], tiles[:, e:e + 1], ALU.add))
            tb(V.tensor_tensor(ge, tile_no.unsqueeze(2).to_broadcast([1, TILES, E]), by_tile(cum), ALU.is_ge))
            tb(V.tensor_reduce(expert, ge, axis=AXX, op=ALU.add))
            tb(V.tensor_tensor(gn, ge, by_tile(tiles), ALU.mult))
            tb(V.tensor_reduce(excl, gn, axis=AXX, op=ALU.add))
            tb(V.tensor_tensor(excl, tile_no, excl, ALU.subtract))
            tb(V.tensor_scalar(row0, expert, float(REGION), None, ALU.mult))
            tb(V.scalar_tensor_tensor(out=row0, in0=excl, scalar=float(P), in1=row0, op0=ALU.mult, op1=ALU.add))
            tb(V.tensor_copy(row0_i[:, :], row0))
            tb(V.tensor_scalar(woff, expert, float(E - 1), float(F), ALU.min, ALU.mult))
            V.tensor_copy(woff_i[:, :], woff).then_inc(s_tab_done, 1)

            def step(t, n, r):
                def inside(t):
                    return not isinstance(t, int) or 0 <= t < TILES

                if inside(t):
                    dve.wait_ge(s_lin, t + 1)
                    dve.wait_ge(s_silu, t + 1)
                    V.tensor_tensor(HH[n % 2], lin_ps[n % 2], SG[n % 2], ALU.mult).then_inc(s_h, 1)
                if inside(t - 1):
                    dve.wait_ge(s_y_ready, t)
                    if not (isinstance(t, int) and t < 4):
                        dve.wait_ge(*rows_out(n - 1 - YRING, r))
                    V.tensor_scalar(YO[(n - 1) % YRING], y_ps[:, 0:D], XG[(n - 1) % RING][:, D + 1:D + 2], None,
                                    ALU.mult).then_inc(s_y, 1)

            tiles_pipeline(dve, step)

            def final(b, n, r):
                dve.wait_ge(s_f_sum, b + 1)
                V.tensor_tensor(X1[n], X1[n], Y0[n], ALU.add).then_inc(s_f_res, 1)
                dve.wait_ge(s_f_res, b + 1)
                for c in range(QC):
                    V.bn_stats(stats[:, c, :], X1[n][:, c, :]).then_inc(s_f_step, 1)
                for c in range(QC):
                    lone_wait(dve, s_f_step, 3 * QC * b + c + 1)
                    V.bn_aggr(meanvar[:, c, :], stats[:, c, :]).then_inc(s_f_step, 1)
                dve.wait_ge(s_f_step, 3 * QC * b + 2 * QC)
                V.tensor_scalar_add(vareps[:, :], meanvar[:, :, 1], EPS).then_inc(s_f_var, 1)
                dve.wait_ge(s_f_rstd, b + 1)
                if not (isinstance(b, int) and b < 2):
                    dve.wait_ge(s_f_stored[n], 16 * r)
                for c in range(QC):
                    last = V.tensor_scalar(RES[n][:, c, :], X1[n][:, c, :], meanvar[:, c, 0:1],
                                           rstd[:, c:c + 1], ALU.subtract, ALU.mult)
                    last.then_inc(s_f_step, 1)

            for n in range(2):
                final(n, n, 0)
            with dve.Fori(1, NB // 2) as i:
                for n in range(2):
                    final(2 * i + n, n, i)

        @block.gpsimd
        def _(pool):
            s_lone[id(pool)] = s_lone_pool
            G = nc.gpsimd
            step_of = [0]

            def cst(ins):
                step_of[0] += 1
                ins.then_inc(s_pool_const, 1)
                pool.wait_ge(s_pool_const, step_of[0])

            cst(G.memset(ones[:, :], 1.0))
            cst(G.affine_select(out=ident[:, :], in_=ones[:, :], compare_op=ALU.is_equal, fill=0.0, base=0,
                                pattern=[[-1, P]], channel_multiplier=1))
            cst(G.affine_select(out=upper[:, :], in_=ones[:, :], compare_op=ALU.is_gt, fill=0.0, base=0,
                                pattern=[[1, P]], channel_multiplier=-1))
            cst(G.memset(minushalf[:, :], -0.5))
            cst(G.iota(rev[:, :, :], pattern=[[0, QC], [-1, E]], base=E, channel_multiplier=0,
                       allow_small_or_imprecise_dtypes=True))
            cst(G.iota(eoff[:, :], pattern=[[REGION // 64, E]], base=0, channel_multiplier=0,
                       allow_small_or_imprecise_dtypes=True))
            cst(G.tensor_scalar(eoff[:, :], eoff[:, :], 64.0, None, ALU.mult))
            cst(G.iota(partition[:, :], pattern=[[0, 1]], base=0, channel_multiplier=1,
                       allow_small_or_imprecise_dtypes=True))
            cst(G.tensor_scalar(notkey0[:, :], partition[:, :], 0.0, None, ALU.is_gt))
            cst(G.iota(dest[:, :, :], pattern=[[NT, 2], [P, QC]], base=0, channel_multiplier=1,
                       allow_small_or_imprecise_dtypes=True))
            cst(G.iota(tab[:, 0, :], pattern=[[1, TILES]], base=0, channel_multiplier=0,
                       allow_small_or_imprecise_dtypes=True))
            cst(G.memset(padrow[:, :], 0.0))
            for n in range(2):
                cst(G.memset(XE[n][:, :, :, :], 0.0))
                cst(G.memset(VE[n][:, :, :, :], 0.0))
                cst(G.memset(VE[n][:, :, :, 2 * DK], 1.0))
                cst(G.memset(VE[n][:, :, :, 2 * DK + 1], 1.0))
                cst(G.tensor_scalar(VE[n][:, 0, :, 2 * DK + 1], VE[n][:, 0, :, 2 * DK + 1], notkey0[:, 0:1],
                                    None, ALU.mult))
            G.memset(rank[:, :], 0.0).then_inc(s_const, 5)

            def split_negmax(b, g):
                u = 4 * b + g
                lone_wait(pool, s_mT_drained, u + 1)
                if not (isinstance(u, int) and u == 0):
                    lone_wait(pool, s_m_stored, 16 * u)
                G.tensor_copy(negmax_parts[:, 0, :], negmax[:, :]).then_inc(s_m_split_step, 1)
                lone_wait(pool, s_m_split_step, u + 1)
                G.tensor_tensor(negmax_parts[:, 1, :], negmax[:, :], negmax_parts[:, 0, :], ALU.subtract)\
                 .then_inc(s_m_split, 1)

            def split_qk(b, which):
                n = 2 * b + which
                lone_wait(pool, s_qk_drained, n + 1)
                if not (isinstance(n, int) and n == 0):
                    lone_wait(pool, s_parts_stored, 16 * n)
                G.tensor_copy(qk_parts[:, 0, :], full[:, :]).then_inc(s_split_step, 1)
                lone_wait(pool, s_split_step, 3 * n + 1)
                G.tensor_tensor(rest[:, :], full[:, :], qk_parts[:, 0, :], ALU.subtract).then_inc(s_split_step, 1)
                lone_wait(pool, s_split_step, 3 * n + 2)
                G.tensor_copy(qk_parts[:, 1, :], rest[:, :]).then_inc(s_split_step, 1)
                lone_wait(pool, s_split_step, 3 * n + 3)
                G.tensor_tensor(qk_parts[:, 2, :], rest[:, :], qk_parts[:, 1, :], ALU.subtract).then_inc(s_split, 1)

            def values_without_key0(b, par):
                lone_wait(pool, s_v_drained, b + 1)
                G.tensor_scalar(VE[par][:, 0, :, DK:2 * DK], VE[par][:, 0, :, 0:DK], notkey0[:, 0:1], None,
                                ALU.mult).then_inc(s_v_step, 1)
                G.tensor_copy(VE[par][:, 1:QC, :, DK:2 * DK], VE[par][:, 1:QC, :, 0:DK]).then_inc(s_v_step, 1)

            def add_bo(b):
                lone_wait(pool, s_x, 16 * (b + 1))
                G.tensor_tensor(x_sb[:, :, :], x_sb[:, :, :],
                                bo_sb[:, :].unsqueeze(1).to_broadcast([P, QC, D]), ALU.add).then_inc(s_xb, 1)

            def send_x(b, par):
                lone_wait(pool, s_xn, b + 1)
                if live(b - 2):
                    lone_wait(pool, s_scattered, SPARE + SENT * (b - 1))
                for s in range(2):
                    G.tensor_copy(XE[par][:, :, s, 0:D], xn[:, :, :]).then_inc(s_sent_step, 1)

            def scatter(b, par):
                lone_wait(pool, s_rt, RT * b + 33)
                lone_wait(pool, s_sent_step, 2 * (b + 1))
                for s in range(2):
                    for c in range(QC):
                        G.indirect_dma_start(rows_d, bass.IndirectOffsetOnAxis(ap=pos[:, s, c:c + 1], axis=0),
                                             XE[par][:, c, s, :], None).then_inc(s_scattered, 16)

            def iteration(b, par):
                for g in range(NG):
                    bb, gg = b + (g + 1) // NG, (g + 1) % NG
                    if g == 3 and live(b - 1):
                        lone_wait(pool, s_var, b)
                        G.tensor_tensor(rstd[:, :], vareps[:, :], minushalf[:, :], ALU.pow).then_inc(s_rstd, 1)
                    if live(bb):
                        split_negmax(bb, gg)
                    if g == 0 and live(b - 1):
                        add_bo(b - 1)
                    if g == 0 and live(b + 2):
                        split_qk(b + 2, 0)
                    if g == 1:
                        if live(b - 2):
                            scatter(b - 2, par)
                        if live(b + 1):
                            values_without_key0(b + 1, 1 - par)
                    if g == 3:
                        if live(b + 2):
                            split_qk(b + 2, 1)
                        if live(b - 1):
                            send_x(b - 1, 1 - par)

            pool.wait_ge(s_weights, s_weights_last)
            pool.wait_ge(s_const_dve, 2)
            for n in range(E):
                r = E * REGION + n * P
                G.dma_start(rows_d[r:r + P, :], padrow[:, :]).then_inc(s_scattered, 16)
            pool.wait_ge(s_scattered, SPARE)
            pipeline(pool, iteration)

            lone_wait(pool, s_rt, RT * NB)
            padf = T1[:, 0, 0, 0:E]
            G.tensor_scalar(padf, offs[:, 0, :], partition[:, 0:1], None, ALU.add).then_inc(s_pad_step, 1)
            lone_wait(pool, s_pad_step, 1)
            G.tensor_copy(padpos[:, :], padf).then_inc(s_pad_step, 1)
            lone_wait(pool, s_pad_step, 2)
            lone_wait(pool, s_const_dve, 2)
            lone_wait(pool, s_scattered, SPARE + SENT * NB)
            for e in range(E):
                G.indirect_dma_start(rows_d, bass.IndirectOffsetOnAxis(ap=padpos[:, e:e + 1], axis=0),
                                     padrow[:, :], None).then_inc(s_pad, 16)

            def step(t, n, r):
                if isinstance(t, int) and not 0 <= t - 1 < TILES:
                    return
                lone_wait(pool, s_y, t)
                G.indirect_dma_start(y_d, bass.IndirectOffsetOnAxis(
                    ap=XG[(n - 1) % RING][:, D:D + 1].bitcast(i32), axis=0), YO[(n - 1) % YRING], None,
                    bounds_check=2 * NT - 1, oob_is_err=False).then_inc(s_y_out[(n - 1) % YRING], 16)

            tiles_pipeline(pool, step)

            def final(b, n, r):
                lone_wait(pool, s_f_in[n], 16 * 3 * (r + 1))
                G.tensor_tensor(Y0[n], Y0[n], Y1[n], ALU.add).then_inc(s_f_sum, 1)
                lone_wait(pool, s_f_var, b + 1)
                G.tensor_tensor(rstd[:, :], vareps[:, :], minushalf[:, :], ALU.pow).then_inc(s_f_rstd, 1)

            for n in range(2):
                final(n, n, 0)
            with pool.Fori(1, NB // 2) as i:
                for n in range(2):
                    final(2 * i + n, n, i)


_SHAPES = {
    "xT": (D, NT), "x": (NT, D), "wqT": (D, D), "wkT": (D, D), "wvT": (D, D), "woT": (D, D),
    "bq": (D, 1), "bk": (D, 1), "bv": (1, D), "bo": (1, D), "gateT": (D, E),
    "w1T": (D, E * F), "w3T": (D, E * F), "w2T": (P, E * F),
}


def kernel(**inputs):
    import concourse.bacc as bacc
    from concourse.bass_utils import run_bass_kernel_spmd

    a = {k.removeprefix("L0_"): np.asarray(v) for k, v in inputs.items()}
    tokens = a["attn_x"].reshape(NT, D)
    w2 = a["ffn_w2"].reshape(E, D, FC, P)
    arrays = {
        "xT": tokens.T, "x": tokens,
        "wqT": a["attn_Wq"].T, "wkT": a["attn_Wk"].T, "wvT": a["attn_Wv"].T, "woT": a["attn_Wo"].T,
        "bq": a["attn_bq"].reshape(D, 1), "bk": a["attn_bk"].reshape(D, 1),
        "bv": a["attn_bv"].reshape(1, D), "bo": a["attn_bo"].reshape(1, D),
        "gateT": a["ffn_gate_w"].T,
        "w1T": a["ffn_w1"].transpose(2, 0, 1).reshape(D, E * F),
        "w3T": a["ffn_w3"].transpose(2, 0, 1).reshape(D, E * F),
        "w2T": w2.transpose(3, 0, 2, 1).reshape(P, E * F),
    }
    arrays = {k: np.ascontiguousarray(v) for k, v in arrays.items()}
    nc = bacc.Bacc("TRN2", target_bir_lowering=False, num_devices=1)
    args = [nc.dram_tensor(k, list(_SHAPES[k]), mybir.dt.float32, kind="ExternalInput").ap() for k in _SHAPES]
    out = nc.dram_tensor("out", [NT, D], mybir.dt.float32, kind="ExternalOutput").ap()
    layer(nc, *args, out)
    r = run_bass_kernel_spmd(nc, [arrays], core_ids=[0])
    return r.results[0]["out"].reshape(NB, L, D)
```

```python
from contextlib import ExitStack

import numpy as np

import concourse.bass as bass
from concourse import mybir

P = 128
NB, L, D = 16, 512, 128
NH = 16
DK = D // NH
NT = NB * L
QC = L // P
HG = 4
NG = NH // HG
VW = 32
PARTS = 3
KR = PARTS * PARTS * DK
MR = 2
E, F = 8, 512
FC = F // P
REGION = NT + P
TILES = 2 * NT // P + E
ROW = 132
SKIP = 1 << 20
EPS = 1e-5
JITTER2 = 0.02
SCALE = float(1.0 / np.sqrt(np.float32(DK)))
BIG = 3.0e38


def layer(nc, xT, x, wqT, wkT, wvT, woT, bq, bk, bv, bo, gateT, w1T, w3T, w2T, out):
    f32, bf16, i32 = mybir.dt.float32, mybir.dt.bfloat16, mybir.dt.int32
    ALU, ACT, AXX = mybir.AluOpType, mybir.ActivationFunctionType, mybir.AxisListType.X

    parts_d = nc.dram_tensor("parts_d", [2, 2, PARTS, P, L], bf16).ap()
    negmax_d = nc.dram_tensor("negmax_d", [2, MR, HG * QC, P], bf16).ap()
    x1_d = nc.dram_tensor("x1_d", [NT, D], f32).ap()
    rows_d = nc.dram_tensor("rows_d", [E * REGION + E * P, ROW], f32).ap()
    y_d = nc.dram_tensor("y_d", [2 * NT, D], f32).ap()

    x_b = x.rearrange("(b c p) d -> b p c d", c=QC, p=P)
    x1_b = x1_d.rearrange("(b c p) d -> b p c d", c=QC, p=P)
    out_b = out.rearrange("(b c p) d -> b p c d", c=QC, p=P)
    y_b = y_d.rearrange("(b c p) d -> b p c d", c=QC, p=P)

    ctx = ExitStack()
    with ctx:
        def sb(name, shape, dt=f32):
            return ctx.enter_context(nc.sbuf_tensor(name + "_sb", shape, dt))

        def sem(name):
            return ctx.enter_context(nc.semaphore(name))

        regions = [sb(f"region{n}", [P, E * F]) for n in range(4)]
        QS = [regions[n][:, :].bitcast(bf16).rearrange("p (h q) -> p h q", h=NH) for n in (0, 1)]
        KS = [regions[n][:, :].bitcast(bf16).rearrange("p (h q) -> p h q", h=NH) for n in (2, 3)]
        W1, W3, W2 = regions[0], regions[2], regions[1]
        pt_flat = [sb(f"probs{n}", [P, HG * QC * L]) for n in range(2)]
        PT = [t[:, :].rearrange("p (j c q) -> p j c q", j=HG, c=QC) for t in pt_flat]
        xT_sb = [sb(f"xT{n}", [D, L]) for n in range(2)]
        x_sb = sb("x", [P, QC, D])
        wq_sb, wk_sb, wv_sb, wo_sb = (sb(n, [D, D]) for n in ("wq", "wk", "wv", "wo"))
        woh_sb = sb("wo_half", [D, D])
        bq_sb, bk_sb = sb("bq", [D, 1]), sb("bk", [D, 1])
        bv_sb, bo_sb = sb("bv", [P, D]), sb("bo", [P, D])
        gate_sb = sb("gate", [D, E])
        ident = sb("ident", [P, P])
        upper = sb("upper", [P, P])
        ones = sb("ones", [P, P])
        full = sb("full", [P, L])
        rest = sb("rest", [P, L])
        qk_parts = sb("qk_parts", [P, PARTS, L], bf16)
        VE = [sb(f"values{n}", [P, QC, NH, VW]) for n in range(2)]
        notkey0 = sb("notkey0", [P, 1])
        rowmax = [sb(f"rowmax{n}", [P, HG * QC]) for n in range(2)]
        negmax = sb("negmax", [HG * QC, P])
        negmax_parts = sb("negmax_parts", [HG * QC, MR, P], bf16)
        OT = sb("OT", [P, L])
        TN = sb("TN", [P, NG, QC, HG, VW])
        recips = sb("recips", [P, 2, NG * QC * HG])
        T1, T2 = (sb(n, [P, NG, QC, HG * DK]) for n in ("T1", "T2"))
        attn = sb("attn", [P, QC, D])
        attnT = sb("attnT", [D, QC, P])
        ysum = sb("ysum", [P, QC, D])
        stats = sb("stats", [P, QC, 6])
        meanvar = sb("meanvar", [P, QC, 2])
        vareps, minushalf, rstd = (sb(n, [P, QC]) for n in ("vareps", "minushalf", "rstd"))
        xn = sb("xn", [P, QC, D])
        xnT = sb("xnT", [D, QC, P])
        logits = sb("logits", [P, QC, E])
        rev = sb("rev", [P, QC, E])
        eoff = sb("eoff", [P, E])
        top = [sb(f"top{n}", [P, QC]) for n in range(2)]
        eqm = sb("eqm", [P, QC, E])
        rank = sb("rank", [P, QC])
        H = sb("H", [P, 2, QC, E])
        Hs = sb("Hs", [P, QC, E])
        l2 = sb("l2", [P, QC, E])
        dist = sb("dist", [P, 2, QC, E])
        absl = sb("absl", [P, QC, E])
        factor = sb("factor", [P, 2, QC, E])
        kept = sb("kept", [P, 2, QC, E])
        expd = sb("expd", [P, 2, QC, E])
        wsum = sb("wsum", [P, 2, QC])
        prefix = sb("prefix", [P, 2, QC, E])
        offs = sb("offs", [P, QC + 1, E])
        posf = sb("posf", [P, 2, QC])
        pos = sb("pos", [P, 2, QC], i32)
        dest = sb("dest", [P, 2, QC])
        XE = [sb(f"sent{n}", [P, QC, 2, ROW]) for n in range(2)]
        padrow = sb("padrow", [P, ROW])
        f_meanvar = sb("final_meanvar", [P, 2, QC, 2])
        f_vareps, f_rstd = sb("final_vareps", [P, 2, QC]), sb("final_rstd", [P, 2, QC])
        partition = sb("partition", [P, 1])
        tab = sb("tab", [1, 5, TILES])
        tabc = sb("tabc", [1, 4, E])
        tabi, end_i = sb("tabi", [1, E], i32), sb("end_i", [1, E], i32)
        row0_i = sb("row0_i", [1, TILES], i32)
        woff_i = sb("woff_i", [1, TILES], i32)

        def psum(name, banks):
            return ctx.enter_context(nc.psum_tensor(name, [P, banks, L], f32))

        st_ps = [psum(f"st_ps{n}", 1) for n in range(3)]
        mx_ps = [psum(f"mx_ps{n}", 1) for n in range(3)]
        acc_ps = psum("acc_ps", 1)
        misc_ps = psum("misc_ps", 1)

        def carve(n, at, words):
            return pt_flat[n][:, at:at + words]

        RING, YRING = 6, 3
        XG = [carve(0, n * ROW, ROW) for n in range(RING)]
        at = RING * ROW
        XGT = [carve(0, at + n * P, P) for n in range(2)]
        at += 2 * P
        SG = [carve(0, at + n * F, F) for n in range(2)]
        at += 2 * F
        HH = [carve(0, at + n * F, F) for n in range(2)]
        at += 2 * F
        HT = [carve(0, at + n * F, F) for n in range(2)]
        at += 2 * F
        YO = [carve(0, at + n * D, D) for n in range(YRING)]
        up_ps = [st_ps[0][:, 0, :], st_ps[1][:, 0, :]]
        lin_ps = [st_ps[2][:, 0, :], mx_ps[2][:, 0, :]]
        xgt_ps, ht_ps, y_ps = mx_ps[0][:, 0, :], mx_ps[1][:, 0, :], misc_ps[:, 0, :]
        tabe = pt_flat[1][0:1, 0:2 * TILES * E].rearrange("p (s t e) -> p s t e", s=2, t=TILES)

        FRING = 4

        def carve3(n, k):
            return carve(1, (n * 4 + k) * L, L).rearrange("p (c d) -> p c d", c=QC)

        Y0, Y1, X1, RES = ([carve3(n, k) for n in range(FRING)] for k in range(4))

        s_weights, s_weights_last = sem("weights"), 16 * 9
        s_const = sem("constants")
        s_ones, s_const_dve = sem("rows_of_ones"), sem("constants_dve")
        s_pool_const = sem("pool_constant")
        s_xT, s_x = sem("xT_loaded"), sem("x_loaded")
        s_qk_ready, s_qk_drained = sem("qk_projected"), sem("qk_drained")
        s_split, s_split_step = sem("qk_split"), sem("qk_split_step")
        s_parts_stored, s_qk_loaded = sem("parts_stored"), sem("qk_loaded")
        s_v_ready, s_v_drained, s_v_step = sem("v_projected"), sem("v_drained"), sem("values_without_key0")
        s_mx_ready, s_mx_done = sem("mx_ready"), sem("mx_done")
        s_mT_ready, s_mT_drained = sem("mT_ready"), sem("mT_drained")
        s_m_split, s_m_split_step = sem("m_split"), sem("m_split_step")
        s_m_stored, s_m_loaded = sem("m_stored"), sem("m_loaded")
        s_st_ready, s_exp_done = sem("st_ready"), sem("exp_done")
        s_pv_ready, s_acc_drained = sem("pv_ready"), sem("acc_drained")
        s_ot_ready, s_ot_drained = sem("ot_ready"), sem("ot_drained")
        s_norm = sem("norm_step")
        s_at_ready, s_at_drained = sem("at_ready"), sem("at_drained")
        s_wo_ready, s_wo_drained = sem("wo_ready"), sem("wo_drained")
        s_xb = sem("x_plus_bo")
        s_ln, s_var, s_rstd = sem("ln_step"), sem("vareps_done"), sem("rstd_done")
        s_xn, s_x1_stored = sem("xn_done"), sem("x1_stored")
        s_xt_ready, s_xt_drained = sem("xt_ready"), sem("xt_drained")
        s_gl_ready, s_gl_drained = sem("gl_ready"), sem("gl_drained")
        s_rt = sem("route_step")
        s_expd = sem("expd_done")
        s_px_ready, s_px_drained = sem("px_ready"), sem("px_drained")
        s_sent_step, s_scattered = sem("sent_x"), sem("scattered")
        s_tab, s_tab_done = sem("table_step"), sem("table_done")
        s_ends, s_pad = sem("expert_ends"), sem("padding_stored")
        s_w = sem("expert_weights")
        s_xg = [sem(f"xg_loaded{n}") for n in range(RING)]
        s_xgt_ready, s_xgt = sem("xgt_ready"), sem("xgt_drained")
        s_up, s_lin, s_silu, s_h = sem("up_ready"), sem("lin_ready"), sem("silu_done"), sem("h_done")
        s_ht_ready, s_ht = sem("ht_ready"), sem("ht_drained")
        s_y_ready, s_y = sem("y_ready"), sem("y_drained")
        s_y_out = [sem(f"y_scattered{n}") for n in range(YRING)]
        s_f_in = [sem(f"final_loaded{n}") for n in range(FRING)]
        s_f_sum, s_f_res = sem("final_ysum"), sem("final_res")
        s_f_step, s_f_var, s_f_rstd = sem("final_step"), sem("final_var"), sem("final_rstd")
        s_f_norm = sem("final_norm")
        s_f_stored = [sem(f"final_stored{n}") for n in range(FRING)]

        s_lone_sp, s_lone_pool, s_lone_dve = (sem(f"lone_waits_{n}") for n in ("sp", "pool", "dve"))
        s_lone = {}

        def live(b):
            return not isinstance(b, int) or 0 <= b < NB

        def bank(i):
            return 1 if i == SC - 1 else i % 3

        def last_use(i):
            return i - 1 - next(k for k in range(1, SC) if bank((i - 1 - k) % SC) == bank(i)) \
                if bank((i - 1) % SC) != bank(i) else i - 1

        def lone_wait(eng, s, n):
            eng.wait_ge(s, n)
            if not isinstance(n, int):
                eng.sem_inc(s_lone[id(eng)], 1)

        def pipeline(eng, iteration):
            for b in range(-2, 2):
                iteration(b, b % 2)
            with eng.Fori(1, NB // 2 - 1) as i:
                iteration(2 * i, 0)
                iteration(2 * i + 1, 1)
            for b in range(NB - 2, NB + 2):
                iteration(b, b % 2)

        def rows_in(n, r):
            return s_xg[n % RING], 16 * (r + n // RING + 1)

        def rows_out(n, r):
            return s_y_out[n % YRING], 16 * (RING // YRING * r + n // YRING + 1)

        def tiles_pipeline(eng, step):
            first = RING
            rounds = (TILES - 1 - first) // RING
            for t in range(-1, first):
                step(t, t % RING, t // RING)
            with eng.Fori(1, 1 + rounds) as i:
                for n in range(RING):
                    step(RING * i + n, n, i)
            for t in range(first + rounds * RING, TILES + 1):
                step(t, t % RING, t // RING)

        SPARE, SENT = 16, 16 * 2 * QC
        def final_pipeline(eng, step):
            first, last = FRING + 1, NB - FRING + 1
            for t in range(first):
                step(t, t % FRING, t // FRING)
            with eng.Fori(1, last // FRING) as i:
                for n in range(1, FRING + 1):
                    step(FRING * i + n, n % FRING, i + n // FRING)
            for t in range(last, NB + 1):
                step(t, t % FRING, t // FRING)

        SC = NH * QC
        NORM, LN, RT = 6, 2 * QC, 33

        block = ctx.enter_context(nc.Block())

        @block.sync
        def _(sp):
            s_lone[id(sp)] = s_lone_sp
            for dst, src in ((wq_sb, wqT), (wk_sb, wkT), (wv_sb, wvT), (wo_sb, woT), (gate_sb, gateT),
                             (bq_sb, bq), (bk_sb, bk)):
                sp.dma_start(dst[:, :], src).then_inc(s_weights, 16)
            sp.dma_start(bv_sb[:, :], bv.to_broadcast([P, D])).then_inc(s_weights, 16)
            sp.dma_start(bo_sb[:, :], bo.to_broadcast([P, D])).then_inc(s_weights, 16)

            def load_xT(b, par):
                if live(b - 2):
                    lone_wait(sp, s_v_ready, b - 1)
                    lone_wait(sp, s_qk_ready, 2 * (b - 1))
                col = b * L
                src = xT[:, col:col + L] if isinstance(b, int) else xT[:, bass.ds(col, L)]
                sp.dma_start(xT_sb[par][:, :], src).then_inc(s_xT, 16)

            def load_x(b):
                if live(b - 1):
                    lone_wait(sp, s_wo_drained, b)
                src = x_b[b] if isinstance(b, int) else x_b[bass.ds(b, 1)].rearrange("o p c d -> (o p) c d")
                sp.dma_start(x_sb[:, :, :], src).then_inc(s_x, 16)

            def store_parts(b, par, which):
                lone_wait(sp, s_split, 2 * b + which + 1)
                if live(b - 2):
                    lone_wait(sp, s_qk_loaded, 16 * 2 * PARTS * PARTS * (b - 1))
                sp.dma_start(parts_d[par, which].rearrange("t p q -> p t q"), qk_parts[:, :, :])\
                  .then_inc(s_parts_stored, 16)

            def load_qk(b, par):
                lone_wait(sp, s_parts_stored, 32 * (b + 1))
                if live(b - 2):
                    lone_wait(sp, s_exp_done, SC * (b - 1))
                else:
                    sp.wait_ge(s_ones, 2)
                for c in range(PARTS * PARTS):
                    for which, dst, part in ((0, QS[par], c // PARTS), (1, KS[par], c % PARTS)):
                        sp.dma_start(dst[DK * c:DK * (c + 1), :, :],
                                     parts_d[par, which, part].rearrange("(h d) q -> d h q", d=DK))\
                          .then_inc(s_qk_loaded, 16)

            def move_negmax(b, bpar, g):
                u = 4 * b + g
                lone_wait(sp, s_m_split, u + 1)
                if not (isinstance(u, int) and u < 2):
                    lone_wait(sp, s_m_loaded, 16 * (u - 1))
                sp.dma_start(negmax_d[g % 2].rearrange("t r q -> r t q"), negmax_parts[:, :, :])\
                  .then_inc(s_m_stored, 16)
                lone_wait(sp, s_m_stored, 16 * (u + 1))
                sp.dma_start(QS[bpar][KR:KR + MR, HG * g:HG * (g + 1), :],
                             negmax_d[g % 2].rearrange("t r q -> t (r q)")
                                            .rearrange("t (h q) -> t h q", h=HG)).then_inc(s_m_loaded, 16)

            def store_x1(b):
                lone_wait(sp, s_xn, b + 1)
                dst = x1_b[b] if isinstance(b, int) else x1_b[bass.ds(b, 1)].rearrange("o p c d -> (o p) c d")
                sp.dma_start(dst, xn[:, :, :]).then_inc(s_x1_stored, 16)

            def iteration(b, par):
                if live(b + 2):
                    load_xT(b + 2, par)
                if live(b - 1):
                    load_x(b - 1)
                for g in range(NG):
                    gg, off = (g + 1) % NG, (g + 1) // NG
                    if live(b + off):
                        move_negmax(b + off, (par + off) % 2, gg)
                    if g == 0 and live(b + 1):
                        load_qk(b + 1, 1 - par)
                    if g == 1 and live(b + 2):
                        store_parts(b + 2, par, 0)
                    if g == 3:
                        if live(b + 2):
                            store_parts(b + 2, par, 1)
                        if live(b - 1):
                            store_x1(b - 1)

            pipeline(sp, iteration)

            sp.wait_ge(s_exp_done, SC * NB)
            for dst, src in ((W1, w1T), (W3, w3T), (W2, w2T)):
                sp.dma_start(dst[:, :], src).then_inc(s_w, 16)
            sp.wait_ge(s_ends, 1)
            for e in range(E):
                end = sp.value_load(end_i[0:1, e:e + 1], min_val=0, max_val=E * REGION - P)
                sp.dma_start(rows_d[bass.ds(end, P), :], padrow[:, :]).then_inc(s_pad, 16)
            sp.wait_ge(s_scattered, SPARE + SENT * NB)
            sp.wait_ge(s_pad, 16 * E)
            sp.wait_ge(s_tab_done, 1)
            sp.wait_ge(s_pv_ready, 4 * NB)

            def load_rows(t, n, r):
                if not (isinstance(t, int) and t < RING):
                    lone_wait(sp, *rows_out(n, r - 1))
                at = row0_i[0:1, t:t + 1] if isinstance(t, int) else row0_i[0:1, bass.ds(t, 1)]
                row = sp.value_load(at, min_val=0, max_val=E * REGION + (E - 1) * P)
                sp.dma_start(XG[n], rows_d[bass.ds(row, P), :]).then_inc(s_xg[n], 16)

            for t in range(RING):
                load_rows(t, t, 0)
            with sp.Fori(1, TILES // RING) as i:
                for n in range(RING):
                    load_rows(RING * i + n, n, i)
            for t in range(TILES // RING * RING, TILES):
                load_rows(t, t % RING, t // RING)

            for t in range(TILES - YRING, TILES):
                sp.wait_ge(*rows_out(t % RING, t // RING))
            sp.wait_ge(s_x1_stored, 16 * NB)

            def final_load(b, n):
                if not (isinstance(b, int) and b < FRING):
                    lone_wait(sp, s_f_norm, QC * (b - FRING + 1))
                for dst, src, k in ((Y0[n], y_b, 0), (Y1[n], y_b, NB), (X1[n], x1_b, 0)):
                    at = src[b + k] if isinstance(b, int) else \
                        src[bass.ds(b + k, 1)].rearrange("o p c d -> (o p) c d")
                    sp.dma_start(dst, at).then_inc(s_f_in[n], 16)

            def final_store(b, n):
                lone_wait(sp, s_f_norm, QC * (b + 1))
                dst = out_b[b] if isinstance(b, int) else out_b[bass.ds(b, 1)].rearrange("o p c d -> (o p) c d")
                sp.dma_start(dst, RES[n]).then_inc(s_f_stored[n], 16)

            for n in range(FRING):
                final_load(n, n)
            with sp.Fori(0, NB // FRING - 1) as i:
                for n in range(FRING):
                    final_store(FRING * i + n, n)
                    final_load(FRING * i + n + FRING, n)
            for n in range(FRING):
                final_store(NB - FRING + n, n)
            for n in range(FRING):
                sp.wait_ge(s_f_stored[n], 16 * (NB // FRING))

        @block.tensor
        def _(pe):
            pieces = []
            for k in range(16):
                g = k // 4
                if k % 4 == 0:
                    pieces.append((s_mT_drained, (g + 1) // NG, 4, (g + 1) % NG))
                elif k % 4 == 1:
                    pieces.append((s_ot_drained, (g - 2) // NG, 4, (g - 2) % NG))
                else:
                    pieces.append({2: (s_px_drained, -2, 1, 0), 3: (s_qk_drained, 2, 2, 0),
                                   6: (s_v_drained, 1, 1, 0), 7: (s_qk_drained, 2, 2, 1),
                                   10: (s_at_drained, -1, 1, 0), 11: (s_wo_drained, -1, 1, 0),
                                   14: (s_xt_drained, -1, 1, 0), 15: (s_gl_drained, -1, 1, 0)}[k])

            def misc_free(b, k):
                for back in range(1, 32):
                    kk, bb = (k - back) % 16, b + (k - back) // 16
                    s, off, per, n = pieces[kk]
                    if live(bb + off):
                        pe.wait_ge(s, per * (bb + off) + n + 1)
                        return

            def bank_free(s, b, i):
                if not (isinstance(b, int) and SC * b + last_use(i) < 0):
                    pe.wait_ge(s, SC * b + last_use(i) + 1)

            def score_chunk(b, par, g, j, c):
                i, h = 16 * g + 4 * j + c, HG * g + j
                bank_free(s_exp_done, b, i)
                nc.tensor.matmul(st_ps[bank(i)][:, 0, :], KS[par][0:KR + MR, h, P * c:P * (c + 1)],
                                 QS[par][0:KR + MR, h, :], start=True, stop=True).then_inc(s_st_ready, 1)

            def max_chunk(b, par, g, j, c):
                i, h = 16 * g + 4 * j + c, HG * g + j
                bank_free(s_mx_done, b, i)
                nc.tensor.matmul(mx_ps[bank(i)][:, 0, :], QS[par][0:KR, h, P * c:P * (c + 1)],
                                 KS[par][0:KR, h, :], start=True, stop=True).then_inc(s_mx_ready, 1)

            def values(b, par, g, j):
                u = 4 * b + g
                if j == 0:
                    if not (isinstance(u, int) and u == 0):
                        pe.wait_ge(s_acc_drained, u)
                    pe.wait_ge(s_exp_done, 16 * (u + 1))
                    pe.wait_ge(s_v_step, 3 * (b + 1))
                for hj in range(HG):
                    last = nc.tensor.matmul(acc_ps[32 * hj:32 * hj + VW, 0, :],
                                            VE[par][:, j, HG * g + hj, :], PT[g % 2][:, hj, j, :],
                                            start=(j == 0), stop=(j == QC - 1))
                if j == QC - 1:
                    last.then_inc(s_pv_ready, 1)

            def project_qk(b, par, which):
                pe.wait_ge(s_xT, 16 * (b + 1))
                nc.tensor.matmul(misc_ps[:, 0, :], (wq_sb, wk_sb)[which][:, :], xT_sb[par][:, :],
                                 start=True, stop=True).then_inc(s_qk_ready, 1)

            def project_v(par):
                for c in range(QC):
                    last = nc.tensor.matmul(misc_ps[:, 0, P * c:P * (c + 1)], xT_sb[par][:, P * c:P * (c + 1)],
                                            wv_sb[:, :], start=True, stop=True)
                last.then_inc(s_v_ready, 1)

            def max_to_rows(b, g):
                pe.wait_ge(s_mx_done, 16 * (4 * b + g + 1))
                nc.tensor.transpose(misc_ps[0:HG * QC, 0, 0:P], rowmax[g % 2][:, :], ident[:, :])\
                  .then_inc(s_mT_ready, 1)

            def sums_by_query(b, g):
                pe.wait_ge(s_acc_drained, 4 * b + g + 1)
                for c in range(QC):
                    last = nc.tensor.transpose(misc_ps[:, 0, P * c:P * (c + 1)], OT[:, P * c:P * (c + 1)],
                                               ident[:, :])
                last.then_inc(s_ot_ready, 1)

            def chunks_transposed(src, ready):
                for c in range(QC):
                    last = nc.tensor.transpose(misc_ps[:, 0, P * c:P * (c + 1)], src[:, c, :], ident[:, :])
                last.then_inc(ready, 1)

            def misc(b, par, k):
                s, off, per, n = pieces[k]
                bb = b + off
                if not live(bb):
                    return
                misc_free(b, k)
                g = k // 4
                if k % 4 == 0:
                    max_to_rows(bb, (g + 1) % NG)
                elif k % 4 == 1:
                    sums_by_query(bb, (g - 2) % NG)
                elif k == 2:
                    pe.wait_ge(s_rt, RT * bb + 12)
                    nc.tensor.matmul(misc_ps[:, 0, 0:QC * E], upper[:, :], Hs[:, :, :], start=True, stop=True)
                    nc.tensor.matmul(misc_ps[:, 0, QC * E:2 * QC * E], ones[:, :], Hs[:, :, :],
                                     start=True, stop=True).then_inc(s_px_ready, 1)
                elif k in (3, 7):
                    project_qk(bb, par, k == 7)
                elif k == 6:
                    project_v(1 - par)
                elif k == 10:
                    pe.wait_ge(s_norm, NORM * (bb + 1))
                    chunks_transposed(attn, s_at_ready)
                elif k == 11:
                    pe.wait_ge(s_at_drained, bb + 1)
                    for c in range(QC):
                        last = nc.tensor.matmul(misc_ps[:, 0, P * c:P * (c + 1)], attnT[:, c, :],
                                                woh_sb[:, :], start=True, stop=True)
                    last.then_inc(s_wo_ready, 1)
                elif k == 14:
                    pe.wait_ge(s_xn, bb + 1)
                    chunks_transposed(xn, s_xt_ready)
                elif k == 15:
                    pe.wait_ge(s_xt_drained, bb + 1)
                    for c in range(QC):
                        last = nc.tensor.matmul(misc_ps[:, 0, E * c:E * (c + 1)], xnT[:, c, :],
                                                gate_sb[:, :], start=True, stop=True)
                    last.then_inc(s_gl_ready, 1)

            def iteration(b, par):
                for k in range(16):
                    g, j = k // 4, k % 4
                    ahead, ga = (g + 2) // NG, (g + 2) % NG
                    behind, gb = (g - 1) // NG, (g - 1) % NG
                    if j == 0 and live(b):
                        pe.wait_ge(s_m_loaded, 16 * (4 * b + g + 1))
                    if live(b + ahead) and ga == 0 and j == 0:
                        pe.wait_ge(s_qk_loaded, 16 * 2 * PARTS * PARTS * (b + ahead + 1))

                    def chunk(c):
                        if live(b + ahead):
                            max_chunk(b + ahead, (par + ahead) % 2, ga, j, c)

                    def scores(c):
                        if live(b):
                            score_chunk(b, par, g, j, c)

                    chunk(0)
                    scores(0)
                    scores(1)
                    chunk(1)
                    if live(b + behind):
                        values(b + behind, (par + behind) % 2, gb, j)
                    chunk(2)
                    scores(2)
                    scores(3)
                    chunk(3)
                    misc(b, par, k)

            pe.wait_ge(s_weights, s_weights_last)
            pe.wait_ge(s_const, 6)
            pipeline(pe, iteration)

            pe.wait_ge(s_tab_done, 1)
            pe.wait_ge(s_w, 16 * 3)
            pe.wait_ge(s_exp_done, SC * NB)

            carried = [pe.alloc_register(f"expert_offset{n}") for n in range(2)]
            limits = dict(min_val=0, max_val=(E - 1) * F)
            offsets = {}

            def load_offset(t, n):
                at = woff_i[0:1, t:t + 1] if isinstance(t, int) else woff_i[0:1, bass.ds(t, 1)]
                if n % RING == 0:
                    pe.reg_load(carried[0], at)
                else:
                    offsets[n] = pe.value_load(at, **limits)

            def weights(w, n, at, width):
                return w[:, bass.ds(offsets[n % RING] + at, width)]

            def inside(t):
                return not isinstance(t, int) or 0 <= t < TILES

            def step(t, n, r):
                if n == 0:
                    offsets[0] = pe.snap(carried[0], **limits)
                    if not (isinstance(t, int) and t == 0):
                        offsets[RING - 1] = pe.snap(carried[1], **limits)
                if inside(t):
                    pe.wait_ge(s_xgt, t + 1)
                    nc.tensor.matmul(up_ps[n % 2], XGT[n % 2], weights(W1, n, 0, F), start=True, stop=True)\
                      .then_inc(s_up, 1)
                if inside(t - 1):
                    pe.wait_ge(s_h, t)
                    for c in range(FC):
                        last = nc.tensor.transpose(ht_ps[:, P * c:P * (c + 1)],
                                                   HH[(n - 1) % 2][:, P * c:P * (c + 1)], ident[:, :])
                    last.then_inc(s_ht_ready, 1)
                if inside(t + 1):
                    pe.wait_ge(*rows_in(n + 1, r))
                    nc.tensor.transpose(xgt_ps[:, 0:P], XG[(n + 1) % RING][:, 0:P], ident[:, :])\
                      .then_inc(s_xgt_ready, 1)
                if inside(t):
                    nc.tensor.matmul(lin_ps[n % 2], XGT[n % 2], weights(W3, n, 0, F), start=True, stop=True)\
                      .then_inc(s_lin, 1)
                if inside(t + 1):
                    load_offset(t + 1, n + 1)
                if inside(t - 1):
                    pe.wait_ge(s_ht, t)
                    if not (isinstance(t, int) and t < 2):
                        pe.wait_ge(s_y, t - 1)
                    for c in range(FC):
                        last = nc.tensor.matmul(y_ps[:, 0:D], HT[(n - 1) % 2][:, P * c:P * (c + 1)],
                                                weights(W2, n - 1, c * D, D), start=(c == 0), stop=(c == FC - 1))
                    last.then_inc(s_y_ready, 1)
                if n == RING - 1 and not (isinstance(t, int) and t < 0):
                    pe.reg_mov(carried[1], offsets[n])

            tiles_pipeline(pe, step)

        @block.scalar
        def _(act):
            act.wait_ge(s_weights, s_weights_last)
            nc.scalar.activation(woh_sb[:, :], wo_sb[:, :], ACT.Copy, scale=0.5).then_inc(s_const, 1)

            def exp_chunk(b, g, j, c):
                i, u = 16 * g + 4 * j + c, 4 * b + g
                if j == 0 and c == 0 and not (isinstance(u, int) and u < 2):
                    act.wait_ge(s_pv_ready, u - 1)
                act.wait_ge(s_st_ready, SC * b + i + 1)
                nc.scalar.activation(PT[g % 2][:, j, c, :], st_ps[bank(i)][:, 0, :],
                                     ACT.Exp, scale=SCALE).then_inc(s_exp_done, 1)

            def drain_sums(b, g):
                u = 4 * b + g
                act.wait_ge(s_pv_ready, u + 1)
                if not (isinstance(u, int) and u == 0):
                    act.wait_ge(s_ot_ready, u)
                nc.scalar.activation(OT[:, :], acc_ps[:, 0, :], ACT.Copy).then_inc(s_acc_drained, 1)

            def drain(b, par, k):
                g = k // 4
                if k % 4 == 0:
                    bb, gg = b + (g + 1) // NG, (g + 1) % NG
                    if live(bb):
                        u = 4 * bb + gg
                        act.wait_ge(s_mT_ready, u + 1)
                        if not (isinstance(u, int) and u == 0):
                            act.wait_ge(s_m_split, u)
                        nc.scalar.activation(negmax[:, :], misc_ps[0:HG * QC, 0, 0:P], ACT.Copy, scale=-1.0)\
                          .then_inc(s_mT_drained, 1)
                elif k % 4 == 1:
                    bb, gg = b + (g - 2) // NG, (g - 2) % NG
                    if live(bb):
                        act.wait_ge(s_ot_ready, 4 * bb + gg + 1)
                        if gg == 0 and live(bb - 1):
                            act.wait_ge(s_norm, NORM * bb)
                        nc.scalar.activation(TN[:, gg, :, :, :], misc_ps[:, 0, :]
                                             .rearrange("p (c j v) -> p c j v", c=QC, j=HG), ACT.Copy)\
                          .then_inc(s_ot_drained, 1)
                elif k == 2 and live(b - 2):
                    act.wait_ge(s_px_ready, b - 1)
                    nc.scalar.activation(prefix[:, :, :, :], misc_ps[:, 0, 0:2 * QC * E]
                                         .rearrange("p (s c e) -> p s c e", s=2, c=QC), ACT.Copy)\
                      .then_inc(s_px_drained, 1)
                elif k in (3, 7) and live(b + 2):
                    which = int(k == 7)
                    n = 2 * (b + 2) + which
                    act.wait_ge(s_qk_ready, n + 1)
                    if not (isinstance(n, int) and n == 0):
                        act.wait_ge(s_split, n)
                    nc.scalar.activation(full[:, :], misc_ps[:, 0, :], ACT.Identity,
                                         bias=(bq_sb, bk_sb)[which][:, 0:1]).then_inc(s_qk_drained, 1)
                elif k == 6 and live(b + 1):
                    act.wait_ge(s_v_ready, b + 2)
                    if isinstance(b, int) and b < 0:
                        act.wait_ge(s_const_dve, 11)
                    if live(b - 1):
                        act.wait_ge(s_pv_ready, 4 * b)
                    nc.scalar.activation(VE[1 - par][:, :, :, DK:2 * DK], misc_ps[:, 0, :]
                                         .rearrange("p (c h d) -> p c h d", c=QC, h=NH), ACT.Copy)\
                      .then_inc(s_v_drained, 1)
                elif k == 10 and live(b - 1):
                    act.wait_ge(s_at_ready, b)
                    nc.scalar.activation(attnT[:, :, :], misc_ps[:, 0, :].rearrange("p (c q) -> p c q", c=QC),
                                         ACT.Copy).then_inc(s_at_drained, 1)
                elif k == 14 and live(b - 1):
                    act.wait_ge(s_xt_ready, b)
                    nc.scalar.activation(xnT[:, :, :], misc_ps[:, 0, :].rearrange("p (c q) -> p c q", c=QC),
                                         ACT.Copy).then_inc(s_xt_drained, 1)
                elif k == 15 and live(b - 1):
                    act.wait_ge(s_gl_ready, b)
                    if live(b - 2):
                        act.wait_ge(s_rt, RT * (b - 1))
                    nc.scalar.activation(logits[:, :, :], misc_ps[:, 0, 0:QC * E]
                                         .rearrange("p (c e) -> p c e", c=QC), ACT.Copy).then_inc(s_gl_drained, 1)

            def iteration(b, par):
                for k in range(16):
                    g, j = k // 4, k % 4
                    if live(b):
                        for c in range(QC):
                            exp_chunk(b, g, j, c)
                    if j == QC - 1 and live(b + (g - 1) // NG):
                        drain_sums(b + (g - 1) // NG, (g - 1) % NG)
                    drain(b, par, k)
                    if k == 2 and live(b - 2):
                        act.wait_ge(s_rt, RT * (b - 2) + 14)
                        nc.scalar.activation(expd[:, :, :, :], dist[:, :, :, :], ACT.Exp, scale=-1.0)\
                          .then_inc(s_expd, 1)

            pipeline(act, iteration)

            def step(t, n, r):
                def inside(t):
                    return not isinstance(t, int) or 0 <= t < TILES

                if inside(t):
                    act.wait_ge(s_up, t + 1)
                    nc.scalar.activation(SG[n % 2], up_ps[n % 2], ACT.Silu).then_inc(s_silu, 1)
                if inside(t - 1):
                    act.wait_ge(s_ht_ready, t)
                    nc.scalar.activation(HT[(n - 1) % 2], ht_ps[:, :], ACT.Copy).then_inc(s_ht, 1)
                if inside(t + 1):
                    act.wait_ge(s_xgt_ready, t + 2)
                    nc.scalar.activation(XGT[(n + 1) % 2], xgt_ps[:, 0:P], ACT.Copy).then_inc(s_xgt, 1)

            tiles_pipeline(act, step)

        @block.vector
        def _(dve):
            s_lone[id(dve)] = s_lone_dve
            V = nc.vector
            step_of = [0]

            def cst(ins):
                step_of[0] += 1
                ins.then_inc(s_const_dve, 1)
                dve.wait_ge(s_const_dve, step_of[0])

            for n in range(2):
                V.memset(KS[n][64:P, :, :], 1.0).then_inc(s_ones, 1)
            dve.wait_ge(s_const, 6)
            cst(V.tensor_copy(offs[:, 0, :], eoff[:, :]))
            for n in range(2):
                cst(V.memset(XE[n][:, :, :, :], 0.0))
                cst(V.memset(VE[n][:, :, :, :], 0.0))
                cst(V.memset(VE[n][:, :, :, 2 * DK], 1.0))
                cst(V.memset(VE[n][:, :, :, 2 * DK + 1], 1.0))
                cst(V.tensor_scalar(VE[n][:, 0, :, 2 * DK + 1], VE[n][:, 0, :, 2 * DK + 1], notkey0[:, 0:1],
                                    None, ALU.mult))

            def after_step(s, n):
                dve.wait_ge(s, n)

            def iteration(b, par):
                count = [0]

                def next_max():
                    k, c = divmod(count[0], QC)
                    count[0] += 1
                    g, j = k // 4, k % 4
                    bb, ga = b + (g + 2) // NG, (g + 2) % NG
                    if not live(bb):
                        return
                    u = 4 * bb + ga
                    if j == 0 and c == 0 and not (isinstance(u, int) and u < 2):
                        dve.wait_ge(s_mT_ready, u - 1)
                    n = 16 * u + 4 * j + c
                    dve.wait_ge(s_mx_ready, n + 1)
                    V.tensor_reduce(rowmax[ga % 2][:, 4 * j + c:4 * j + c + 1], mx_ps[bank(16 * ga + 4 * j + c)][:, 0, :],
                                    axis=AXX, op=ALU.max).then_inc(s_mx_done, 1)

                rb = b - 2
                route = live(rb)
                H1, H2 = H[:, 0, :, :], H[:, 1, :, :]

                def rt(n):
                    dve.wait_ge(s_rt, RT * rb + n)

                def per_chunk(x):
                    return x[:, :].unsqueeze(2).to_broadcast([P, QC, E])

                next_max()
                if route:
                    dve.wait_ge(s_gl_drained, rb + 1)
                    V.tensor_reduce(top[0][:, :], logits[:, :, :], axis=AXX, op=ALU.max).then_inc(s_rt, 1)
                next_max()
                if route:
                    rt(1)
                    V.tensor_tensor(eqm[:, :, :], logits[:, :, :], per_chunk(top[0]), ALU.is_equal).then_inc(s_rt, 1)
                    rt(2)
                    V.tensor_tensor(absl[:, :, :], eqm[:, :, :], rev[:, :, :], ALU.mult).then_inc(s_rt, 1)
                next_max()
                if route:
                    rt(3)
                    V.tensor_reduce(rank[:, :], absl[:, :, :], axis=AXX, op=ALU.max).then_inc(s_rt, 1)
                    rt(4)
                    V.tensor_tensor(H1, absl[:, :, :], per_chunk(rank), ALU.is_equal).then_inc(s_rt, 1)
                next_max()
                if route:
                    rt(5)
                    V.scalar_tensor_tensor(out=l2[:, :, :], in0=H1, scalar=-BIG, in1=logits[:, :, :],
                                           op0=ALU.mult, op1=ALU.add).then_inc(s_rt, 1)
                    rt(6)
                    V.tensor_reduce(top[1][:, :], l2[:, :, :], axis=AXX, op=ALU.max).then_inc(s_rt, 1)
                next_max()
                if route:
                    rt(7)
                    V.tensor_tensor(eqm[:, :, :], l2[:, :, :], per_chunk(top[1]), ALU.is_equal).then_inc(s_rt, 1)
                    rt(8)
                    V.tensor_tensor(absl[:, :, :], eqm[:, :, :], rev[:, :, :], ALU.mult).then_inc(s_rt, 1)
                next_max()
                if route:
                    rt(9)
                    V.tensor_reduce(rank[:, :], absl[:, :, :], axis=AXX, op=ALU.max).then_inc(s_rt, 1)
                    rt(10)
                    V.tensor_tensor(H2, absl[:, :, :], per_chunk(rank), ALU.is_equal).then_inc(s_rt, 1)
                next_max()
                if route:
                    rt(11)
                    V.tensor_tensor(Hs[:, :, :], H1, H2, ALU.add).then_inc(s_rt, 1)
                    V.scalar_tensor_tensor(out=dist[:, 0, :, :], in0=logits[:, :, :], scalar=-1.0,
                                           in1=per_chunk(top[0]), op0=ALU.mult, op1=ALU.add).then_inc(s_rt, 1)
                    V.scalar_tensor_tensor(out=dist[:, 1, :, :], in0=l2[:, :, :], scalar=-1.0,
                                           in1=per_chunk(top[1]), op0=ALU.mult, op1=ALU.add).then_inc(s_rt, 1)
                next_max()
                next_max()
                if route:
                    V.scalar_tensor_tensor(out=absl[:, :, :], in0=logits[:, :, :], scalar=-1.0,
                                           in1=logits[:, :, :], op0=ALU.mult, op1=ALU.max).then_inc(s_rt, 1)
                    rt(15)
                    for s in range(2):
                        V.tensor_tensor(factor[:, s, :, :], absl[:, :, :], per_chunk(top[s]), ALU.max)\
                         .then_inc(s_rt, 1)
                if route:
                    rt(17)
                    V.scalar_tensor_tensor(out=kept[:, :, :, :], in0=factor[:, :, :, :], scalar=JITTER2,
                                           in1=dist[:, :, :, :], op0=ALU.mult, op1=ALU.is_ge).then_inc(s_rt, 1)
                next_max()
                next_max()
                next_max()
                if route:
                    rt(18)
                    dve.wait_ge(s_expd, rb + 1)
                    V.tensor_tensor(factor[:, :, :, :], kept[:, :, :, :], expd[:, :, :, :], ALU.mult)\
                     .then_inc(s_rt, 1)
                next_max()
                if route:
                    rt(19)
                    V.tensor_reduce(wsum[:, :, :], factor[:, :, :, :], axis=AXX, op=ALU.add).then_inc(s_rt, 1)
                    rt(20)
                    if live(rb - 1):
                        dve.wait_ge(s_scattered, SPARE + SENT * rb)
                    V.reciprocal(XE[par][:, :, :, D + 1].rearrange("p c s -> p s c"), wsum[:, :, :])\
                     .then_inc(s_rt, 1)
                    V.tensor_copy(XE[par][:, :, :, D].bitcast(i32).rearrange("p c s -> p s c"), dest[:, :, :])\
                     .then_inc(s_rt, 1)
                next_max()
                if route:
                    rt(22)
                    V.tensor_scalar_add(dest[:, :, :], dest[:, :, :], float(L)).then_inc(s_rt, 1)

                for c in range(QC):
                    next_max()
                    if route:
                        if c == 0:
                            dve.wait_ge(s_px_drained, rb + 1)
                            rt(23)
                        else:
                            rt(23 + c)
                        V.tensor_tensor(offs[:, c + 1, :], offs[:, c, :], prefix[:, 1, c, :], ALU.add)\
                         .then_inc(s_rt, 1)
                next_max()
                if route:
                    rt(27)
                    V.tensor_tensor(l2[:, :, :], prefix[:, 0, :, :], offs[:, 0:QC, :], ALU.add).then_inc(s_rt, 1)
                    rt(28)
                    for s in range(2):
                        V.tensor_tensor(factor[:, s, :, :], H[:, s, :, :], l2[:, :, :], ALU.mult).then_inc(s_rt, 1)
                next_max()
                if route:
                    rt(30)
                    V.tensor_reduce(posf[:, :, :], factor[:, :, :, :], axis=AXX, op=ALU.add).then_inc(s_rt, 1)
                    V.tensor_copy(offs[:, 0, :], offs[:, QC, :]).then_inc(s_rt, 1)
                    rt(32)
                    V.tensor_copy(pos[:, :, :], posf[:, :, :]).then_inc(s_rt, 1)
                nb = b - 1
                norm = live(nb)
                SUMS = TN[:, :, :, :, :].rearrange("p g c j v -> p (g c j) v")
                z, z2 = SUMS[:, :, 2 * DK], SUMS[:, :, 2 * DK + 1]
                r1, r2 = recips[:, 0, :], recips[:, 1, :]

                for c in range(QC):
                    next_max()
                next_max()
                if norm:
                    dve.wait_ge(s_ot_drained, 4 * (nb + 1))
                    V.scalar_tensor_tensor(out=r2, in0=z, scalar=1e-9, in1=z2, op0=ALU.mult, op1=ALU.max)\
                     .then_inc(s_norm, 1)
                    V.reciprocal(r1, z).then_inc(s_norm, 1)
                next_max()
                if norm:
                    after_step(s_norm, NORM * nb + 1)
                    V.reciprocal(r2, r2).then_inc(s_norm, 1)
                next_max()
                next_max()
                for c in range(QC):
                    next_max()
                for c in range(3 * QC):
                    next_max()
                for c in range(QC):
                    next_max()
                next_max()
                if norm:
                    dve.wait_ge(s_wo_ready, nb + 1)
                    dve.wait_ge(s_xb, nb + 1)
                    V.tensor_tensor(ysum[:, :, :], misc_ps[:, 0, :].rearrange("p (c d) -> p c d", c=QC),
                                    x_sb[:, :, :], ALU.add).then_inc(s_wo_drained, 1)
                for c in range(QC):
                    next_max()
                    if norm:
                        if c == 0:
                            dve.wait_ge(s_wo_drained, nb + 1)
                        V.bn_stats(stats[:, c, :], ysum[:, c, :]).then_inc(s_ln, 1)
                if norm:
                    for c in range(QC):
                        lone_wait(dve, s_ln, LN * nb + c + 1)
                        V.bn_aggr(meanvar[:, c, :], stats[:, c, :]).then_inc(s_ln, 1)
                    dve.wait_ge(s_ln, LN * (nb + 1))
                    V.tensor_scalar_add(vareps[:, :], meanvar[:, :, 1], EPS).then_inc(s_var, 1)
                next_max()
                next_max()
                next_max()
                if norm:
                    dve.wait_ge(s_rstd, nb + 1)
                    if live(nb - 1):
                        dve.wait_ge(s_x1_stored, 16 * nb)
                        dve.wait_ge(s_xt_ready, nb)
                        dve.wait_ge(s_sent_step, 2 * nb)
                    for c in range(QC):
                        last = V.tensor_scalar(xn[:, c, :], ysum[:, c, :], meanvar[:, c, 0:1], rstd[:, c:c + 1],
                                               ALU.subtract, ALU.mult)
                        if c == 1:
                            next_max()
                    last.then_inc(s_xn, 1)
                while count[0] < 64:
                    next_max()

            pipeline(dve, iteration)

            step_of = [0]

            def tb(ins):
                step_of[0] += 1
                ins.then_inc(s_tab, 1)
                dve.wait_ge(s_tab, step_of[0])

            V.tensor_copy(end_i[:, :], offs[0:1, 0, :]).then_inc(s_ends, 1)
            cnt, tiles, cum = tabc[:, 0, :], tabc[:, 1, :], tabc[:, 2, :]
            tile_no, expert, excl, row0, woff = (tab[:, n, :] for n in range(5))
            ge, gn = tabe[:, 0, :, :], tabe[:, 1, :, :]

            def by_tile(x):
                return x.unsqueeze(1).to_broadcast([1, TILES, E])

            dve.wait_ge(s_pv_ready, 4 * NB)
            tb(V.tensor_tensor(cnt, offs[0:1, 0, :], eoff[0:1, :], ALU.subtract))
            tb(V.tensor_scalar_add(cnt, cnt, float(P - 1)))
            tb(V.tensor_copy(tabi[:, :], cnt))
            tb(V.tensor_scalar(tabi[:, :], tabi[:, :], P.bit_length() - 1, None, ALU.logical_shift_right))
            tb(V.tensor_copy(tiles, tabi[:, :]))
            tb(V.tensor_copy(cum[:, 0:1], tiles[:, 0:1]))
            for e in range(1, E):
                tb(V.tensor_tensor(cum[:, e:e + 1], cum[:, e - 1:e], tiles[:, e:e + 1], ALU.add))
            tb(V.tensor_tensor(ge, tile_no.unsqueeze(2).to_broadcast([1, TILES, E]), by_tile(cum), ALU.is_ge))
            tb(V.tensor_reduce(expert, ge, axis=AXX, op=ALU.add))
            tb(V.tensor_tensor(gn, ge, by_tile(tiles), ALU.mult))
            tb(V.tensor_reduce(excl, gn, axis=AXX, op=ALU.add))
            tb(V.tensor_tensor(excl, tile_no, excl, ALU.subtract))
            tb(V.tensor_scalar(row0, expert, float(REGION), None, ALU.mult))
            tb(V.scalar_tensor_tensor(out=row0, in0=excl, scalar=float(P), in1=row0, op0=ALU.mult, op1=ALU.add))
            tb(V.tensor_copy(row0_i[:, :], row0))
            tb(V.tensor_scalar(woff, expert, float(E - 1), float(F), ALU.min, ALU.mult))
            V.tensor_copy(woff_i[:, :], woff).then_inc(s_tab_done, 1)

            def step(t, n, r):
                def inside(t):
                    return not isinstance(t, int) or 0 <= t < TILES

                if inside(t):
                    dve.wait_ge(s_lin, t + 1)
                    dve.wait_ge(s_silu, t + 1)
                    V.tensor_tensor(HH[n % 2], lin_ps[n % 2], SG[n % 2], ALU.mult).then_inc(s_h, 1)
                if inside(t - 1):
                    dve.wait_ge(s_y_ready, t)
                    if not (isinstance(t, int) and t < 4):
                        dve.wait_ge(*rows_out(n - 1 - YRING, r))
                    V.tensor_scalar(YO[(n - 1) % YRING], y_ps[:, 0:D], XG[(n - 1) % RING][:, D + 1:D + 2], None,
                                    ALU.mult).then_inc(s_y, 1)

            tiles_pipeline(dve, step)

            def residual_stats(b, n):
                dve.wait_ge(s_f_sum, b + 1)
                V.tensor_tensor(X1[n], X1[n], Y0[n], ALU.add).then_inc(s_f_res, 1)
                dve.wait_ge(s_f_res, b + 1)
                for c in range(QC):
                    V.bn_stats(stats[:, c, :], X1[n][:, c, :]).then_inc(s_f_step, 1)
                for c in range(QC):
                    lone_wait(dve, s_f_step, 2 * QC * b + c + 1)
                    V.bn_aggr(f_meanvar[:, n % 2, c, :], stats[:, c, :]).then_inc(s_f_step, 1)
                dve.wait_ge(s_f_step, 2 * QC * (b + 1))
                V.tensor_scalar_add(f_vareps[:, n % 2, :], f_meanvar[:, n % 2, :, 1], EPS).then_inc(s_f_var, 1)

            def final_norm(b, n, r):
                dve.wait_ge(s_f_rstd, b + 1)
                if not (isinstance(b, int) and b < FRING):
                    dve.wait_ge(s_f_stored[n], 16 * r)
                for c in range(QC):
                    V.tensor_scalar(RES[n][:, c, :], X1[n][:, c, :], f_meanvar[:, n % 2, c, 0:1],
                                    f_rstd[:, n % 2, c:c + 1], ALU.subtract, ALU.mult).then_inc(s_f_norm, 1)

            def step(b, n, r):
                if not (isinstance(b, int) and b == NB):
                    residual_stats(b, n)
                if not (isinstance(b, int) and b == 0):
                    final_norm(b - 1, (n - 1) % FRING, r if n else r - 1)

            final_pipeline(dve, step)

        @block.gpsimd
        def _(pool):
            s_lone[id(pool)] = s_lone_pool
            G = nc.gpsimd
            step_of = [0]

            def cst(ins):
                step_of[0] += 1
                ins.then_inc(s_pool_const, 1)
                pool.wait_ge(s_pool_const, step_of[0])

            cst(G.memset(ones[:, :], 1.0))
            cst(G.affine_select(out=ident[:, :], in_=ones[:, :], compare_op=ALU.is_equal, fill=0.0, base=0,
                                pattern=[[-1, P]], channel_multiplier=1))
            cst(G.affine_select(out=upper[:, :], in_=ones[:, :], compare_op=ALU.is_gt, fill=0.0, base=0,
                                pattern=[[1, P]], channel_multiplier=-1))
            cst(G.memset(minushalf[:, :], -0.5))
            cst(G.iota(rev[:, :, :], pattern=[[0, QC], [-1, E]], base=E, channel_multiplier=0,
                       allow_small_or_imprecise_dtypes=True))
            cst(G.iota(eoff[:, :], pattern=[[REGION // 64, E]], base=0, channel_multiplier=0,
                       allow_small_or_imprecise_dtypes=True))
            cst(G.tensor_scalar(eoff[:, :], eoff[:, :], 64.0, None, ALU.mult))
            cst(G.iota(partition[:, :], pattern=[[0, 1]], base=0, channel_multiplier=1,
                       allow_small_or_imprecise_dtypes=True))
            cst(G.tensor_scalar(notkey0[:, :], partition[:, :], 0.0, None, ALU.is_gt))
            cst(G.iota(dest[:, :, :], pattern=[[NT, 2], [P, QC]], base=0, channel_multiplier=1,
                       allow_small_or_imprecise_dtypes=True))
            cst(G.iota(tab[:, 0, :], pattern=[[1, TILES]], base=0, channel_multiplier=0,
                       allow_small_or_imprecise_dtypes=True))
            cst(G.memset(padrow[:, :], 0.0))
            cst(G.memset(padrow[:, D:D + 1].bitcast(i32), SKIP))
            G.memset(rank[:, :], 0.0).then_inc(s_const, 5)

            def split_negmax(b, g):
                u = 4 * b + g
                lone_wait(pool, s_mT_drained, u + 1)
                if not (isinstance(u, int) and u == 0):
                    lone_wait(pool, s_m_stored, 16 * u)
                G.tensor_copy(negmax_parts[:, 0, :], negmax[:, :]).then_inc(s_m_split_step, 1)
                lone_wait(pool, s_m_split_step, u + 1)
                G.tensor_tensor(negmax_parts[:, 1, :], negmax[:, :], negmax_parts[:, 0, :], ALU.subtract)\
                 .then_inc(s_m_split, 1)

            def split_qk(b, which):
                n = 2 * b + which
                lone_wait(pool, s_qk_drained, n + 1)
                if not (isinstance(n, int) and n == 0):
                    lone_wait(pool, s_parts_stored, 16 * n)
                G.tensor_copy(qk_parts[:, 0, :], full[:, :]).then_inc(s_split_step, 1)
                lone_wait(pool, s_split_step, 3 * n + 1)
                G.tensor_tensor(rest[:, :], full[:, :], qk_parts[:, 0, :], ALU.subtract).then_inc(s_split_step, 1)
                lone_wait(pool, s_split_step, 3 * n + 2)
                G.tensor_copy(qk_parts[:, 1, :], rest[:, :]).then_inc(s_split_step, 1)
                lone_wait(pool, s_split_step, 3 * n + 3)
                G.tensor_tensor(qk_parts[:, 2, :], rest[:, :], qk_parts[:, 1, :], ALU.subtract).then_inc(s_split, 1)

            def values_without_key0(b, par):
                lone_wait(pool, s_v_drained, b + 1)
                if isinstance(b, int) and b == 0:
                    pool.wait_ge(s_weights, s_weights_last)
                G.tensor_tensor(VE[par][:, :, :, 0:DK], VE[par][:, :, :, DK:2 * DK],
                                bv_sb[:, :].rearrange("p (h d) -> p h d", h=NH).unsqueeze(1)
                                           .to_broadcast([P, QC, NH, DK]), ALU.add).then_inc(s_v_step, 1)
                lone_wait(pool, s_v_step, 3 * b + 1)
                G.tensor_scalar(VE[par][:, 0, :, DK:2 * DK], VE[par][:, 0, :, 0:DK], notkey0[:, 0:1], None,
                                ALU.mult).then_inc(s_v_step, 1)
                G.tensor_copy(VE[par][:, 1:QC, :, DK:2 * DK], VE[par][:, 1:QC, :, 0:DK]).then_inc(s_v_step, 1)

            def normalise(b):
                SUMS = TN[:, :, :, :, :].rearrange("p g c j v -> p (g c j) v")

                def by_head(t):
                    return t[:, :, :, :].rearrange("p g c (j d) -> p (g c j) d", d=DK)

                def per_head(n):
                    return recips[:, n, :].unsqueeze(2).to_broadcast([P, NG * QC * HG, DK])

                lone_wait(pool, s_norm, NORM * b + 3)
                G.tensor_tensor(by_head(T1), SUMS[:, :, 0:DK], per_head(0), ALU.mult).then_inc(s_norm, 1)
                G.tensor_tensor(by_head(T2), SUMS[:, :, DK:2 * DK], per_head(1), ALU.mult).then_inc(s_norm, 1)
                lone_wait(pool, s_norm, NORM * b + 5)
                G.tensor_tensor(attn[:, :, :].rearrange("p c (g n) -> p g c n", g=NG), T1[:, :, :, :],
                                T2[:, :, :, :], ALU.add).then_inc(s_norm, 1)

            def add_bo(b):
                lone_wait(pool, s_x, 16 * (b + 1))
                if isinstance(b, int) and b == 0:
                    pool.wait_ge(s_weights, s_weights_last)
                G.tensor_tensor(x_sb[:, :, :], x_sb[:, :, :],
                                bo_sb[:, :].unsqueeze(1).to_broadcast([P, QC, D]), ALU.add).then_inc(s_xb, 1)

            def send_x(b, par):
                lone_wait(pool, s_xn, b + 1)
                if live(b - 2):
                    lone_wait(pool, s_scattered, SPARE + SENT * (b - 1))
                for s in range(2):
                    G.tensor_copy(XE[par][:, :, s, 0:D], xn[:, :, :]).then_inc(s_sent_step, 1)

            def scatter(b, par):
                lone_wait(pool, s_rt, RT * b + 33)
                lone_wait(pool, s_sent_step, 2 * (b + 1))
                for s in range(2):
                    for c in range(QC):
                        G.indirect_dma_start(rows_d, bass.IndirectOffsetOnAxis(ap=pos[:, s, c:c + 1], axis=0),
                                             XE[par][:, c, s, :], None).then_inc(s_scattered, 16)

            def iteration(b, par):
                for g in range(NG):
                    bb, gg = b + (g + 1) // NG, (g + 1) % NG
                    if g == 3 and live(b - 1):
                        lone_wait(pool, s_var, b)
                        G.tensor_tensor(rstd[:, :], vareps[:, :], minushalf[:, :], ALU.pow).then_inc(s_rstd, 1)
                    if live(bb):
                        split_negmax(bb, gg)
                    if g == 0 and live(b - 1):
                        add_bo(b - 1)
                    if g == 0 and live(b + 2):
                        split_qk(b + 2, 0)
                    if g == 1:
                        if live(b - 1):
                            normalise(b - 1)
                        if live(b + 1):
                            values_without_key0(b + 1, 1 - par)
                    if g == 2 and live(b - 2):
                        scatter(b - 2, par)
                    if g == 3:
                        if live(b + 2):
                            split_qk(b + 2, 1)
                        if live(b - 1):
                            send_x(b - 1, 1 - par)

            r = E * REGION
            G.dma_start(rows_d[r:r + E * P, :].rearrange("(e p) w -> p e w", p=P),
                        padrow[:, :].unsqueeze(1).to_broadcast([P, E, ROW])).then_inc(s_scattered, 16)
            pipeline(pool, iteration)

            def step(t, n, r):
                if isinstance(t, int) and not 0 <= t - 1 < TILES:
                    return
                lone_wait(pool, s_y, t)
                G.indirect_dma_start(y_d, bass.IndirectOffsetOnAxis(
                    ap=XG[(n - 1) % RING][:, D:D + 1].bitcast(i32), axis=0), YO[(n - 1) % YRING], None,
                    bounds_check=2 * NT - 1, oob_is_err=False).then_inc(s_y_out[(n - 1) % YRING], 16)

            tiles_pipeline(pool, step)

            def step(b, n, r):
                if not (isinstance(b, int) and b == NB):
                    lone_wait(pool, s_f_in[n], 16 * 3 * (r + 1))
                    G.tensor_tensor(Y0[n], Y0[n], Y1[n], ALU.add).then_inc(s_f_sum, 1)
                if not (isinstance(b, int) and b == 0):
                    lone_wait(pool, s_f_var, b)
                    G.tensor_tensor(f_rstd[:, (n - 1) % 2, :], f_vareps[:, (n - 1) % 2, :], minushalf[:, :],
                                    ALU.pow).then_inc(s_f_rstd, 1)

            final_pipeline(pool, step)


_SHAPES = {
    "xT": (D, NT), "x": (NT, D), "wqT": (D, D), "wkT": (D, D), "wvT": (D, D), "woT": (D, D),
    "bq": (D, 1), "bk": (D, 1), "bv": (1, D), "bo": (1, D), "gateT": (D, E),
    "w1T": (D, E * F), "w3T": (D, E * F), "w2T": (P, E * F),
}


def kernel(**inputs):
    import concourse.bacc as bacc
    from concourse.bass_utils import run_bass_kernel_spmd

    a = {k.removeprefix("L0_"): np.asarray(v) for k, v in inputs.items()}
    tokens = a["attn_x"].reshape(NT, D)
    w2 = a["ffn_w2"].reshape(E, D, FC, P)
    arrays = {
        "xT": tokens.T, "x": tokens,
        "wqT": a["attn_Wq"].T, "wkT": a["attn_Wk"].T, "wvT": a["attn_Wv"].T, "woT": a["attn_Wo"].T,
        "bq": a["attn_bq"].reshape(D, 1), "bk": a["attn_bk"].reshape(D, 1),
        "bv": a["attn_bv"].reshape(1, D), "bo": a["attn_bo"].reshape(1, D),
        "gateT": a["ffn_gate_w"].T,
        "w1T": a["ffn_w1"].transpose(2, 0, 1).reshape(D, E * F),
        "w3T": a["ffn_w3"].transpose(2, 0, 1).reshape(D, E * F),
        "w2T": w2.transpose(3, 0, 2, 1).reshape(P, E * F),
    }
    arrays = {k: np.ascontiguousarray(v) for k, v in arrays.items()}
    nc = bacc.Bacc("TRN2", target_bir_lowering=False, num_devices=1)
    args = [nc.dram_tensor(k, list(_SHAPES[k]), mybir.dt.float32, kind="ExternalInput").ap() for k in _SHAPES]
    out = nc.dram_tensor("out", [NT, D], mybir.dt.float32, kind="ExternalOutput").ap()
    layer(nc, *args, out)
    r = run_bass_kernel_spmd(nc, [arrays], core_ids=[0])
    return r.results[0]["out"].reshape(NB, L, D)
```
